# Optimizing a Trainium2 kernel written in Bass

```python
import numpy as np
import jax
import jax.numpy as jnp

def _softmax(x, axis=-1):
    return jax.nn.softmax(x, axis=axis)

def _gelu(x):
    return jax.nn.gelu(x, approximate=True)

def _silu(x):
    return jax.nn.silu(x)

def _sigmoid(x):
    return jax.nn.sigmoid(x)

def _layernorm(x, axis=-1, eps=1e-05):
    m = jnp.mean(x, axis=axis, keepdims=True)
    v = jnp.var(x, axis=axis, keepdims=True)
    return (x - m) / jnp.sqrt(v + eps)

def _scatter_add(tgt, idx, src, axis=0):
    return tgt.at[idx].add(src)

def _segment_sum(src, seg, n):
    return jax.ops.segment_sum(src, seg, n)
kernel_name = 'mk_xattn_seq_d2_seqx_r2_d02176'

def setup_inputs(seed: int=0):
    np.random.seed(seed)
    _w = jnp.asarray

    def _rec_inputs():
        import jax
        import jax.numpy as jnp
        _rk = jax.random.key(seed)
        x = -0.0002928 + 1 * jax.random.normal(jax.random.fold_in(_rk, 1), (8, 1024, 512), jnp.float32)
        _lenS = 1024 - jax.random.randint(jax.random.fold_in(_rk, 7), (8,), 0, max(1, 1024 // 4) + 1, jnp.int32)
        _lenS2 = 64 - jax.random.randint(jax.random.fold_in(_rk, 8), (8,), 0, max(1, 64 // 4) + 1, jnp.int32)
        _ctx_1024P = jax.random.normal(jax.random.fold_in(_rk, 11), (8, 16, 512), jnp.float32)
        _ctx_1024c = jax.random.dirichlet(jax.random.fold_in(_rk, 511), 0.3 * jnp.ones((16,), jnp.float32), (8, 64))
        _ctx_1024t = jnp.einsum('bsk,bkd->bsd', _ctx_1024c, _ctx_1024P)
        _ctx_1024t = _ctx_1024t * jax.lax.rsqrt(jnp.mean(jnp.square(_ctx_1024t)) + 1e-12) * 0.953939
        ctx_1024 = -1.52775e-05 + 0.999936 * (_ctx_1024t + 0.3 * jax.random.normal(jax.random.fold_in(_rk, 611), (8, 64, 512), jnp.float32))
        return (x, ctx_1024)
    x, ctx_1024 = _rec_inputs()

    def _L0_xattn_setup():
        import jax, jax.numpy as jnp
        import numpy as np
        DIM = 512
        NUM_HEADS = 16
        HEAD_DIM = DIM // NUM_HEADS
        FF = 4 * DIM
        B, T, S = (8, 256, 2048)

        def _perceiver_layer(x, inp, Wq, bq, Wk, bk, Wv, bv, Wo, bo, W1, b1, W2, b2):
            b, t, _ = x.shape
            s = inp.shape[1]
            q = (x @ Wq + bq).reshape(b, t, NUM_HEADS, HEAD_DIM)
            k = (inp @ Wk + bk).reshape(b, s, NUM_HEADS, HEAD_DIM)
            v = (inp @ Wv + bv).reshape(b, s, NUM_HEADS, HEAD_DIM)
            attn = jnp.einsum('bthd,bshd->bhts', q, k)
            attn = jax.nn.softmax(attn / jnp.sqrt(jnp.float32(HEAD_DIM)), axis=-1)
            out = jnp.einsum('bhts,bshd->bthd', attn, v).reshape(b, t, DIM)
            attn_out = out @ Wo + bo
            x = x + attn_out
            h = jax.nn.gelu(x @ W1 + b1, approximate=True)
            x = x + (h @ W2 + b2)
            return x
        key = jax.random.key(seed)
        ks = jax.random.split(key, 14)
        sc = 1.0 / np.sqrt(DIM)
        inp = {'x': jax.random.normal(ks[0], (B, T, DIM), jnp.float32), 'inp': jax.random.normal(ks[1], (B, S, DIM), jnp.float32), 'Wq': jax.random.normal(ks[2], (DIM, DIM), jnp.float32) * sc, 'bq': jnp.zeros((DIM,), jnp.float32), 'Wk': jax.random.normal(ks[3], (DIM, DIM), jnp.float32) * sc, 'bk': jnp.zeros((DIM,), jnp.float32), 'Wv': jax.random.normal(ks[4], (DIM, DIM), jnp.float32) * sc, 'bv': jnp.zeros((DIM,), jnp.float32), 'Wo': jax.random.normal(ks[5], (DIM, DIM), jnp.float32) * sc, 'bo': jnp.zeros((DIM,), jnp.float32), 'W1': jax.random.normal(ks[6], (DIM, FF), jnp.float32) * sc, 'b1': jnp.zeros((FF,), jnp.float32), 'W2': jax.random.normal(ks[7], (FF, DIM), jnp.float32) * (1.0 / np.sqrt(FF)), 'b2': jnp.zeros((DIM,), jnp.float32)}
        return inp
    _L0_xattn_all = _L0_xattn_setup()
    _L0_xattn_in = {k: v for k, v in _L0_xattn_all.items() if k in ('Wq', 'bq', 'Wk', 'bk', 'Wv', 'bv', 'Wo', 'bo', 'W1', 'b1', 'W2', 'b2')}
    del _L0_xattn_all

    def _L1_xattn_setup():
        import jax, jax.numpy as jnp
        import numpy as np
        NUM_UNITS = 512
        NUM_HEADS = 16
        CAUSALITY = True
        EPS = 1e-08
        NEG = jnp.float32(-2 ** 32 + 1)

        def _split_heads(x, H):
            B, S, U = x.shape
            d = U // H
            return x.reshape(B, S, H, d).transpose(2, 0, 1, 3).reshape(H * B, S, d)

        def _merge_heads(x, H):
            HB, S, d = x.shape
            B = HB // H
            return x.reshape(H, B, S, d).transpose(1, 2, 0, 3).reshape(B, S, H * d)

        def _layer_norm(x, gamma, beta):
            mean = jnp.mean(x, axis=-1, keepdims=True)
            std = jnp.std(x, axis=-1, keepdims=True, ddof=1)
            return gamma * (x - mean) / (std + EPS) + beta
        key = jax.random.key(seed)
        ks = jax.random.split(key, 12)
        B, S, U = (2, 1024, NUM_UNITS)
        s = 1.0 / np.sqrt(U)
        return {'queries': jax.random.normal(ks[0], (B, S, U), jnp.float32), 'keys': jax.random.normal(ks[1], (B, S, U), jnp.float32), 'values': jax.random.normal(ks[2], (B, S, U), jnp.float32), 'Wq': jax.random.normal(ks[3], (U, U), jnp.float32) * s, 'bq': jax.random.normal(ks[4], (U,), jnp.float32) * s, 'Wk': jax.random.normal(ks[5], (U, U), jnp.float32) * s, 'bk': jax.random.normal(ks[6], (U,), jnp.float32) * s, 'Wv': jax.random.normal(ks[7], (U, U), jnp.float32) * s, 'bv': jax.random.normal(ks[8], (U,), jnp.float32) * s, 'gamma': jnp.ones((U,), jnp.float32), 'beta': jnp.zeros((U,), jnp.float32)}
    _L1_xattn_all = _L1_xattn_setup()
    _L1_xattn_in = {k: v for k, v in _L1_xattn_all.items() if k in ('Wq', 'bq', 'Wk', 'bk', 'Wv', 'bv', 'gamma', 'beta')}
    del _L1_xattn_all
    return {'x': x, 'ctx_1024': ctx_1024, 'L0_xattn_Wq': _L0_xattn_in['Wq'], 'L0_xattn_bq': _L0_xattn_in['bq'], 'L0_xattn_Wk': _L0_xattn_in['Wk'], 'L0_xattn_bk': _L0_xattn_in['bk'], 'L0_xattn_Wv': _L0_xattn_in['Wv'], 'L0_xattn_bv': _L0_xattn_in['bv'], 'L0_xattn_Wo': _L0_xattn_in['Wo'], 'L0_xattn_bo': _L0_xattn_in['bo'], 'L0_xattn_W1': _L0_xattn_in['W1'], 'L0_xattn_b1': _L0_xattn_in['b1'], 'L0_xattn_W2': _L0_xattn_in['W2'], 'L0_xattn_b2': _L0_xattn_in['b2'], 'L1_xattn_Wq': _L1_xattn_in['Wq'], 'L1_xattn_bq': _L1_xattn_in['bq'], 'L1_xattn_Wk': _L1_xattn_in['Wk'], 'L1_xattn_bk': _L1_xattn_in['bk'], 'L1_xattn_Wv': _L1_xattn_in['Wv'], 'L1_xattn_bv': _L1_xattn_in['bv'], 'L1_xattn_gamma': _L1_xattn_in['gamma'], 'L1_xattn_beta': _L1_xattn_in['beta']}

def reference(x, ctx_1024, L0_xattn_Wq, L0_xattn_bq, L0_xattn_Wk, L0_xattn_bk, L0_xattn_Wv, L0_xattn_bv, L0_xattn_Wo, L0_xattn_bo, L0_xattn_W1, L0_xattn_b1, L0_xattn_W2, L0_xattn_b2, L1_xattn_Wq, L1_xattn_bq, L1_xattn_Wk, L1_xattn_bk, L1_xattn_Wv, L1_xattn_bv, L1_xattn_gamma, L1_xattn_beta):
    import jax
    import jax.numpy as jnp

    def _L0_xattn_ref(x, inp, Wq, bq, Wk, bk, Wv, bv, Wo, bo, W1, b1, W2, b2):
        import jax, jax.numpy as jnp
        import numpy as np
        DIM = 512
        NUM_HEADS = 16
        HEAD_DIM = DIM // NUM_HEADS
        FF = 4 * DIM
        B, T, S = (8, 256, 2048)

        def _perceiver_layer(x, inp, Wq, bq, Wk, bk, Wv, bv, Wo, bo, W1, b1, W2, b2):
            b, t, _ = x.shape
            s = inp.shape[1]
            q = (x @ Wq + bq).reshape(b, t, NUM_HEADS, HEAD_DIM)
            k = (inp @ Wk + bk).reshape(b, s, NUM_HEADS, HEAD_DIM)
            v = (inp @ Wv + bv).reshape(b, s, NUM_HEADS, HEAD_DIM)
            attn = jnp.einsum('bthd,bshd->bhts', q, k)
            attn = jax.nn.softmax(attn / jnp.sqrt(jnp.float32(HEAD_DIM)), axis=-1)
            out = jnp.einsum('bhts,bshd->bthd', attn, v).reshape(b, t, DIM)
            attn_out = out @ Wo + bo
            x = x + attn_out
            h = jax.nn.gelu(x @ W1 + b1, approximate=True)
            x = x + (h @ W2 + b2)
            return x
        return _perceiver_layer(x, inp, Wq, bq, Wk, bk, Wv, bv, Wo, bo, W1, b1, W2, b2)

    def _L1_xattn_ref(queries, keys, values, Wq, bq, Wk, bk, Wv, bv, gamma, beta):
        import jax, jax.numpy as jnp
        import numpy as np
        NUM_UNITS = 512
        NUM_HEADS = 16
        CAUSALITY = True
        EPS = 1e-08
        NEG = jnp.float32(-2 ** 32 + 1)

        def _split_heads(x, H):
            B, S, U = x.shape
            d = U // H
            return x.reshape(B, S, H, d).transpose(2, 0, 1, 3).reshape(H * B, S, d)

        def _merge_heads(x, H):
            HB, S, d = x.shape
            B = HB // H
            return x.reshape(H, B, S, d).transpose(1, 2, 0, 3).reshape(B, S, H * d)

        def _layer_norm(x, gamma, beta):
            mean = jnp.mean(x, axis=-1, keepdims=True)
            std = jnp.std(x, axis=-1, keepdims=True, ddof=1)
            return gamma * (x - mean) / (std + EPS) + beta
        H = NUM_HEADS
        B, Sq, U = queries.shape
        Sk = keys.shape[1]
        d = U // H
        Q = jax.nn.relu(queries @ Wq.T + bq)
        K = jax.nn.relu(keys @ Wk.T + bk)
        V = jax.nn.relu(values @ Wv.T + bv)
        Q_ = _split_heads(Q, H)
        K_ = _split_heads(K, H)
        V_ = _split_heads(V, H)
        scores = jnp.einsum('bqd,bkd->bqk', Q_, K_) / jnp.sqrt(jnp.float32(d))
        key_mask = jnp.sign(jnp.abs(jnp.sum(keys, axis=-1)))
        key_mask = jnp.tile(key_mask, (H, 1))[:, None, :]
        scores = jnp.where(key_mask == 0.0, NEG, scores)
        if CAUSALITY:
            tril = jnp.tril(jnp.ones((Sq, Sk), jnp.float32))
            scores = jnp.where(tril[None] == 0.0, NEG, scores)
        attn = jax.nn.softmax(scores, axis=-1)
        query_mask = jnp.sign(jnp.abs(jnp.sum(queries, axis=-1)))
        query_mask = jnp.tile(query_mask, (H, 1))[:, :, None]
        attn = attn * query_mask
        out = jnp.einsum('bqk,bkd->bqd', attn, V_)
        out = _merge_heads(out, H)
        out = out + queries
        return _layer_norm(out, gamma, beta)
    x = _L0_xattn_ref(x, ctx_1024, L0_xattn_Wq, L0_xattn_bq, L0_xattn_Wk, L0_xattn_bk, L0_xattn_Wv, L0_xattn_bv, L0_xattn_Wo, L0_xattn_bo, L0_xattn_W1, L0_xattn_b1, L0_xattn_W2, L0_xattn_b2)
    x = _L1_xattn_ref(x, ctx_1024, ctx_1024, L1_xattn_Wq, L1_xattn_bq, L1_xattn_Wk, L1_xattn_bk, L1_xattn_Wv, L1_xattn_bv, L1_xattn_gamma, L1_xattn_beta)
    return x

_drawn_inputs = setup_inputs


def setup_inputs(seed=0):
    import zlib

    import numpy as np

    out = dict(_drawn_inputs(seed))
    spreads = {'L0_xattn_bq': (0.0, 0.414),
     'L0_xattn_bk': (0.0, 2.0),
     'L0_xattn_bv': (0.0, 0.1),
     'L0_xattn_bo': (0.0, 0.1),
     'L0_xattn_b1': (0.0, 0.1),
     'L0_xattn_b2': (0.0, 0.1),
     'L1_xattn_gamma': (1.0, 0.2),
     'L1_xattn_beta': (0.0, 0.1)}
    factors = {'L1_xattn_bq': 31.077, 'L1_xattn_bk': 34.171, 'L1_xattn_bv': 3.633}
    for name, (base, spread) in spreads.items():
        noise = np.random.default_rng([zlib.crc32(name.encode()), seed]).standard_normal(out[name].shape)
        drawn = base * np.exp(spread * noise) if base else spread * noise
        out[name] = jnp.asarray(drawn.astype(out[name].dtype))
    for name, factor in factors.items():
        out[name] = (out[name] * factor).astype(out[name].dtype)
    return out
```

```python
from contextlib import ExitStack

import concourse.bass as bass
from concourse import mybir

F32 = mybir.dt.float32
F32R = mybir.dt.float32r
ALU = mybir.AluOpType
ACT = mybir.ActivationFunctionType
AX_X = mybir.AxisListType.X

P = 128
DIM = 512
C = DIM // P
HEADS = 16
HD = DIM // HEADS
FF = 4 * DIM
J = FF // P
B = 8
S = 64
TOK = 1024
N = 512
TPB = TOK // N
NT = B * TPB
QB = N // P
HC = P // HD
PAIRS = HEADS // 2
BS = B * S
HALF = HEADS * S // 2
SCALE = 1.0 / float(HD) ** 0.5
NEG = -4294967295.0 * float(HD) ** 0.5
EPS = 1e-8


def wait(eng, sem, value):
    if not isinstance(value, int) or value > 0:
        eng.wait_ge(sem, value)


def over_tiles(eng, body, last_step):
    for t in range(TPB):
        body(t)
    with eng.Fori(1, B - 1) as b:
        for u in range(TPB):
            body(b * TPB + u, u)
    for t in range(NT - TPB, NT):
        body(t)
    if last_step:
        body(NT)


def build_keys(nc, io, persist, scratch):
    with ExitStack() as ctx:
        def sb(name, shape, dt=F32):
            return ctx.enter_context(nc.sbuf_tensor(name, shape, dt))

        def sem(name):
            return ctx.enter_context(nc.semaphore(name))

        ctx_raw = sb("kv_ctx_raw", [P, C, BS])
        ctx_hi = sb("kv_ctx_hi", [P, C, BS], F32R)
        ctx_lo = sb("kv_ctx_lo", [P, C, BS], F32R)
        w_raw = sb("kv_w_raw", [P, 2, C, DIM])
        w_hi = sb("kv_w_hi", [P, 2, C, DIM], F32R)
        w_lo = sb("kv_w_lo", [P, 2, C, DIM], F32R)
        bv = sb("kv_bv", [P, 2, DIM])
        ones = sb("kv_ones", [P, P])
        keep = sb("kv_keep", [P, BS])
        full = sb("kv_full", [P, 2, DIM])
        out_hi = sb("kv_out_hi", [P, 2, DIM], F32R)
        out_lo = sb("kv_out_lo", [P, 2, DIM], F32R)
        acc = ctx.enter_context(nc.psum_tensor("kv_acc", [P, 4, DIM], F32))

        small_in = sem("kv_small_in")
        ctx_in = sem("kv_ctx_in")
        w_in = [sem("kv_w_in0"), sem("kv_w_in1")]
        ones_set = sem("kv_ones_set")
        ctx_split_hi = sem("kv_ctx_split_hi")
        ctx_split_lo = sem("kv_ctx_split_lo")
        w_split_hi = sem("kv_w_split_hi")
        w_split_lo = sem("kv_w_split_lo")
        rows_summed = sem("kv_rows_summed")
        keep_made = sem("kv_keep_made")
        neg_made = sem("kv_neg_made")
        group_ready = sem("kv_group_ready")
        group_read = sem("kv_group_read")
        masked = sem("kv_masked")
        hi_made = sem("kv_hi_made")
        lo_made = sem("kv_lo_made")
        stored = [sem("kv_stored0"), sem("kv_stored1")]
        bk = persist["bk"]
        weights = [io["wk0"], io["wv0"], io["wk1"], io["wv1"], io["wq0"], io["wo0"]]
        NW = len(weights)
        KV = 4
        GROUPS = KV * C

        block = ctx.enter_context(nc.Block())

        @block.sync
        def _(sp):
            sp.dma_start(ctx_raw[:], io["ctxT"].rearrange("(c p) n -> p c n", p=P)).then_inc(ctx_in, 16)
            sp.dma_start(persist["bias"][:], io["bias"]).then_inc(small_in, 16)
            sp.dma_start(bv[:], io["bv"]).then_inc(small_in, 16)
            sp.dma_start(persist["ident"][:], io["ident"]).then_inc(small_in, 16)

            def load_weight(i):
                sp.dma_start(w_raw[:, i % 2], weights[i].rearrange("(c p) n -> p c n", p=P)).then_inc(w_in[i % 2], 16)

            load_weight(0)
            load_weight(1)
            for g in range(GROUPS):
                i, m = g // C, g % C
                if m == 0:
                    sp.wait_ge(w_split_lo, i + 1)
                    load_weight(i + 2)
                layer = i // 2
                sp.wait_ge(lo_made, g + 1)
                for part, src in ((0, out_hi), (1, out_lo)):
                    if i % 2 == 0:
                        dst = scratch["k"][layer, part, m]
                    else:
                        dst = scratch["v"][layer, part, m * P:(m + 1) * P, :]
                    sp.dma_start(dst, src[:, g % 2].bitcast(F32)).then_inc(stored[g % 2], 16)
            for s in range(2):
                sp.wait_ge(stored[s], 16 * 2 * GROUPS // 2)
            sp.wait_ge(small_in, 48)

        @block.scalar
        def _(act):
            act.wait_ge(ctx_in, 16)
            act.activation(ctx_hi[:], ctx_raw[:], ACT.Copy).then_inc(ctx_split_hi, 1)
            for i in range(NW):
                act.wait_ge(w_in[i % 2], 16 * (i // 2 + 1))
                if i < KV:
                    if i >= 2:
                        act.wait_ge(group_ready, C * (i - 1))
                    dst = w_hi[:, i % 2]
                else:
                    dst = persist["wq_hi"][:] if i == KV else persist["wo_hi"][:]
                act.activation(dst, w_raw[:, i % 2], ACT.Copy).then_inc(w_split_hi, 1)

        @block.gpsimd
        def _(pool):
            pool.memset(ones[:], 1.0).then_inc(ones_set, 1)
            pool.memset(persist["zeros"][:], 0.0).then_inc(ones_set, 1)

        @block.vector
        def _(dve):
            dve.wait_ge(ctx_split_hi, 1)
            dve.tensor_tensor(ctx_lo[:], ctx_raw[:], ctx_hi[:], ALU.subtract).then_inc(ctx_split_lo, 1)

            def split_weight(i):
                dve.wait_ge(w_split_hi, i + 1)
                if i < KV:
                    if i >= 2:
                        dve.wait_ge(group_ready, C * (i - 1))
                    lo, hi = w_lo[:, i % 2], w_hi[:, i % 2]
                else:
                    lo, hi = (persist["wq_lo"], persist["wq_hi"]) if i == KV else (persist["wo_lo"], persist["wo_hi"])
                    lo, hi = lo[:], hi[:]
                dve.tensor_tensor(lo, w_raw[:, i % 2], hi, ALU.subtract).then_inc(w_split_lo, 1)

            split_weight(0)
            split_weight(1)
            dve.wait_ge(rows_summed, 1)
            dve.tensor_scalar(keep[:], acc[:, 3], 0.0, None, ALU.not_equal).then_inc(keep_made, 1)
            dve.wait_ge(keep_made, 1)
            dve.tensor_scalar(persist["neg_row"][:], keep[0:1, :], -NEG, NEG, ALU.mult, ALU.add).then_inc(neg_made, 1)
            dve.wait_ge(small_in, 48)
            for g in range(GROUPS):
                i, m = g // C, g % C
                slot = g % 2
                if g % C == 0 and g:
                    if i + 1 < KV:
                        split_weight(i + 1)
                dve.wait_ge(group_ready, g + 1)
                a = acc[:, slot]
                f = full[:, slot]
                if i % 2 == 0:
                    dve.tensor_scalar(f, a, bk[i // 2][:, m:m + 1], 0.0 if i else None,
                                      ALU.add, ALU.max if i else ALU.bypass).then_inc(group_read, 1)
                else:
                    dve.tensor_tensor(f, a, bv[:, i // 2, :], ALU.add).then_inc(group_read, 1)
                dve.wait_ge(group_read, g + 1)
                if i == 2:
                    dve.tensor_tensor(f, f, keep[:], ALU.mult).then_inc(masked, 1)
                    dve.wait_ge(masked, m + 1)
                if i == 3:
                    dve.tensor_scalar(f, f, 0.0, None, ALU.max).then_inc(masked, 1)
                    dve.wait_ge(masked, C + m + 1)
                if g >= 2:
                    dve.wait_ge(stored[slot], 32 * (g // 2))
                dve.tensor_copy(out_hi[:, slot], f).then_inc(hi_made, 1)
                dve.wait_ge(hi_made, g + 1)
                dve.tensor_tensor(out_lo[:, slot], f, out_hi[:, slot], ALU.subtract).then_inc(lo_made, 1)
            split_weight(4)
            split_weight(5)

        @block.tensor
        def _(pe):
            pe.wait_ge(ctx_in, 16)
            pe.wait_ge(ones_set, 1)
            for c in range(C):
                mm = pe.matmul(acc[:, 3], ones[:], ctx_raw[:, c], start=(c == 0), stop=(c == C - 1))
            mm.then_inc(rows_summed, 1)
            pe.wait_ge(ctx_split_lo, 1)
            for g in range(GROUPS):
                i, m = g // C, g % C
                if m == 0:
                    pe.wait_ge(w_split_lo, i + 1)
                if g >= 2:
                    pe.wait_ge(group_read, g - 1)
                n = 0
                for c in range(C):
                    for xw in ((w_hi, ctx_hi), (w_hi, ctx_lo), (w_lo, ctx_hi)):
                        w, x = xw[0][:, i % 2, c], xw[1][:, c]
                        if i % 2 == 0:
                            mm = pe.matmul(acc[:, g % 2], w[:, m * P:(m + 1) * P], x, start=(n == 0), stop=(n == 11))
                        else:
                            mm = pe.matmul(acc[:, g % 2], x[:, m * P:(m + 1) * P], w, start=(n == 0), stop=(n == 11))
                        n += 1
                mm.then_inc(group_ready, 1)


def build_attention(nc, io, persist, scratch, layer):
    second = layer == 1
    x_dram = (scratch["x2"] if second else io["xT"]).rearrange("(c p) n -> p c n", p=P)
    y_dram = io["out"].rearrange("(t b p) n -> t p b n", b=QB, p=P) if second else \
        scratch["x1"].rearrange("(c p) n -> p c n", p=P)
    USES = 14 if second else 12
    HEAD = 6 if second else 4

    with ExitStack() as ctx:
        def sb(name, shape, dt=F32):
            return ctx.enter_context(nc.sbuf_tensor(f"at{layer}_{name}", shape, dt))

        def sem(name):
            return ctx.enter_context(nc.semaphore(f"at{layer}_{name}"))

        x_in = sb("x_in", [P, C, N])
        x_hi = sb("x_hi", [P, C, N], F32R)
        x_lo = sb("x_lo", [P, C, N], F32R)
        q_hi = sb("q_hi", [P, C, N], F32R)
        q_lo = sb("q_lo", [P, C, N], F32R)
        probs = sb("probs", [P, 2, HEADS * S])
        pT_hi = sb("pT_hi", [P, PAIRS, N], F32R)
        pT_lo = sb("pT_lo", [P, PAIRS, N], F32R)
        x_res = sb("x_res", [P, 2, C, N])
        k_hl = sb("k_hl", [P, 2, C, HC * S], F32R)
        v_hl = sb("v_hl", [P, 2, C, 2, P], F32R)
        row_max = sb("row_max", [P, 2, HEADS])
        row_sum = sb("row_sum", [P, 2, HEADS])
        row_inv = sb("row_inv", [P, 2, HEADS])
        acc = ctx.enter_context(nc.psum_tensor(f"at{layer}_acc", [P, 2, N], F32))
        scores = ctx.enter_context(nc.psum_tensor(f"at{layer}_scores", [P, 2, 2 * HALF], F32))
        turned = ctx.enter_context(nc.psum_tensor(f"at{layer}_turned", [P, 2, 4, P], F32))
        ident = persist["ident"]
        bq = persist["bq"][layer]
        if second:
            wq_hi = sb("wq_hi", [P, C, DIM], F32R)
            wq_lo = sb("wq_lo", [P, C, DIM], F32R)
            q_full = sb("q_full", [P, 2, N])
            x_part = sb("x_part", [P, 2, N])
            q_keep = sb("q_keep", [P, 2, QB])
            ones = sb("ones", [P, 2])
            ones_f = sb("ones_f", [1, P])
            ones_r = sb("ones_r", [1, P], F32R)
            neg_r = sb("neg_r", [1, HEADS * S], F32R)
            tri = sb("tri", [P, 2, S])
            gb = sb("gb", [P, 2, DIM])
            normed = sb("normed", [P, 2, DIM])
            stats = sb("stats", [P, QB, 6])
            mean_var = sb("mean_var", [P, QB, 2])
            ln = sb("ln", [P, 4, QB])
            half = sb("half", [P, QB])
            wait_slot = sb("wait_slot", [P, 1])
            out_sb = sb("out_sb", [P, QB, DIM])
        else:
            wq_hi, wq_lo = persist["wq_hi"], persist["wq_lo"]
            wo_hi, wo_lo = persist["wo_hi"], persist["wo_lo"]
            o_hi = sb("o_hi", [P, C, N], F32R)
            o_lo = sb("o_lo", [P, C, N], F32R)

        x_loaded = sem("x_loaded")
        res_loaded = [sem("res_loaded0"), sem("res_loaded1")]
        k_loaded = sem("k_loaded")
        v_loaded = sem("v_loaded")
        out_stored = [sem("out_stored0"), sem("out_stored1")]
        setup_in = sem("setup_in")
        consts_set = sem("consts_set")
        wq_hi_made = sem("wq_hi_made")
        wq_lo_made = sem("wq_lo_made")
        ones_r_made = sem("ones_r_made")
        kv_zeroed = sem("kv_zeroed")
        x_hi_made = sem("x_hi_made")
        x_lo_made = sem("x_lo_made")
        acc_ready = sem("acc_ready")
        acc_hi = sem("acc_hi")
        acc_read = sem("acc_read")
        scores_ready = sem("scores_ready")
        max_made = sem("max_made")
        shifted = sem("shifted")
        exp_made = sem("exp_made")
        sum_made = sem("sum_made")
        inv_made = sem("inv_made")
        probs_ready = sem("probs_ready")
        turned_ready = sem("turned_ready")
        pT_hi_made = sem("pT_hi_made")
        pT_lo_made = sem("pT_lo_made")
        if second:
            part_made = sem("part_made")
            relu_made = sem("relu_made")
            causal_made = sem("causal_made")
            inv_raw = sem("inv_raw")
            turned_out = sem("turned_out")
            stats_made = sem("stats_made")
            ln_step = sem("ln_step")
            sc_step = sem("sc_step")
            neg_set = sem("neg_set")
            root_made = sem("root_made")
            ln_ready = sem("ln_ready")
            normed_made = sem("normed_made")
            gamma_made = sem("gamma_made")
            beta_made = sem("beta_made")

        def absent(t, turns):
            return turns if isinstance(t, int) and t == NT else 0

        def turn(t, k):
            return 2 * HEAD + USES * (t - 1) + k - absent(t, HEAD)

        def head_turn(t, k):
            if isinstance(t, int) and t <= 1:
                return HEAD * t + k
            return turn(t - 1, 8 + k)

        OUT_TURNS = QB if second else 0

        def dve_reads_through(t, k):
            base = 2 * HEAD + (USES - OUT_TURNS) * (t - 1) - absent(t, HEAD)
            if not second:
                return base + k + 1
            return base + (k + 1 if k < 4 else k + 1 - OUT_TURNS)

        def head_reads_through(t, k):
            if isinstance(t, int) and t <= 1:
                return HEAD * t + k + 1
            return dve_reads_through(t - 1, 8 + k)

        def hi_reads_through(t, k):
            return 2 * 4 + 8 * (t - 1) + k - absent(t, 4)

        def bank_free(pe, t, k):
            if k >= 2:
                if second and 4 <= k - 2 < 8:
                    wait(pe, turned_out, QB * (t - 1) + (k - 2 - 4) + 1)
                else:
                    wait(pe, acc_read, dve_reads_through(t, k - 2))
            elif not absent(t, 1):
                wait(pe, acc_read, head_reads_through(t, HEAD + k - 2))
            elif second:
                wait(pe, turned_out, QB * (t - 2) + QB - 2 + k + 1)
            else:
                wait(pe, acc_read, dve_reads_through(t - 1, 6 + k))

        block = ctx.enter_context(nc.Block())

        @block.sync
        def _(sp):
            if second:
                sp.dma_start(x_res[:, 0], io["wq1"].rearrange("(c p) n -> p c n", p=P)).then_inc(setup_in, 16)
                sp.dma_start(tri[:], io["tri"]).then_inc(setup_in, 16)
                sp.dma_start(gb[:], io["gb"]).then_inc(setup_in, 16)

            def load_x(t):
                cols = bass.ds(t * N, N) if not isinstance(t, int) else slice(t * N, (t + 1) * N)
                sp.dma_start(x_in[:], x_dram[:, :, cols]).then_inc(x_loaded, 16)

            load_x(0)
            sp.wait_ge(kv_zeroed, 1)

            def load_k(b):
                src = scratch["k"][layer].rearrange("l c p (b s) -> b p l c s", s=S)[b]
                for h in range(HC):
                    for part in range(2):
                        sp.dma_start(k_hl[h * HD:(h + 1) * HD, part, :, h * S:(h + 1) * S].bitcast(F32),
                                     src[h * HD:(h + 1) * HD, part]).then_inc(k_loaded, 16)

            def load_v(b):
                src = scratch["v"][layer].rearrange("l (b s) (c e g d) -> b e g s l c d", s=S, e=2, g=2, d=HD)[b]
                for e in range(2):
                    for g in range(2):
                        for part in range(2):
                            sp.dma_start(v_hl[g * S:(g + 1) * S, part, :, e,
                                              (2 * e + g) * HD:(2 * e + g + 1) * HD].bitcast(F32),
                                         src[e, g][:, part]).then_inc(v_loaded, 16)

            def body(t, u=None):
                u = t % 2 if u is None else u
                last = isinstance(t, int) and t == NT
                if not isinstance(t, int) or t + 1 < NT:
                    sp.wait_ge(x_lo_made, t + 1)
                    if second:
                        sp.wait_ge(part_made, 3 * t + 2)
                    load_x(t + 1)
                if u == 0 and not last:
                    wait(sp, scores_ready, QB * t)
                    load_k((t // 2) if isinstance(t, int) else t // 2)
                if not last:
                    if second and isinstance(t, int) and t == 0:
                        sp.wait_ge(wq_lo_made, 1)
                    if second:
                        if not isinstance(t, int) or t > 1:
                            sp.wait_ge(acc_ready, turn(t - 1, 7) + 1)
                    else:
                        wait(sp, out_stored[u], 16 * ((t - u) // 2))
                    cols = bass.ds(t * N, N) if not isinstance(t, int) else slice(t * N, (t + 1) * N)
                    sp.dma_start(x_res[:, u], x_dram[:, :, cols]).then_inc(res_loaded[u], 16)
                if u == 0 and not last:
                    if not isinstance(t, int) or t > 0:
                        sp.wait_ge(acc_ready, turn(t, 3) + 1)
                    load_v(t // 2)
                if isinstance(t, int) and t == 0:
                    return
                if second:
                    sp.wait_ge(beta_made, QB * t)
                    sp.dma_start(y_dram[t - 1], out_sb[:]).then_inc(out_stored[0], 16)
                else:
                    sp.wait_ge(acc_read, dve_reads_through(t, 7))
                    cols = bass.ds((t - 1) * N, N) if not isinstance(t, int) else slice((t - 1) * N, t * N)
                    sp.dma_start(y_dram[:, :, cols], x_res[:, 1 - u]).then_inc(out_stored[1 - u], 16)

            over_tiles(sp, body, True)
            if second:
                sp.wait_ge(out_stored[0], 16 * NT)
            else:
                for u in range(2):
                    sp.wait_ge(out_stored[u], 16 * NT // 2)

        @block.gpsimd
        def _(pool):
            pool.memset(k_hl[:].bitcast(F32), 0.0)
            last = pool.memset(v_hl[:].bitcast(F32), 0.0)
            last.then_inc(kv_zeroed, 1)
            if second:
                pool.memset(ones[:], 1.0)
                pool.memset(ones_f[:], 1.0)
                pool.memset(half[:], 0.5).then_inc(consts_set, 1)

            def split_x(t):
                pool.wait_ge(x_hi_made, t + 1)
                if not isinstance(t, int) or t >= 1:
                    pool.wait_ge(acc_ready, head_turn(t - 1, HEAD - 1) + 1)
                pool.tensor_tensor(x_lo[:], x_in[:], x_hi[:], ALU.subtract).then_inc(x_lo_made, 1)
                if second:
                    pool.tensor_tensor(x_part[:, 0], x_in[:, 0], x_in[:, 1], ALU.add).then_inc(part_made, 1)
                    pool.tensor_tensor(x_part[:, 1], x_in[:, 2], x_in[:, 3], ALU.add).then_inc(part_made, 1)
                    pool.wait_ge(part_made, 3 * t + 2)
                    pool.tensor_tensor(x_part[:, 0], x_part[:, 0], x_part[:, 1], ALU.add).then_inc(part_made, 1)

            split_x(0)

            def body(t, u=None):
                last = isinstance(t, int) and t == NT
                for b in range(QB):
                    if not last:
                        g = QB * t + b
                        pool.wait_ge(inv_made, g + 1)
                        p3 = probs[:, b % 2].rearrange("p (h s) -> p h s", s=S)
                        pool.tensor_tensor(p3, p3, row_inv[:, b % 2].unsqueeze(2).to_broadcast([P, HEADS, S]),
                                           ALU.mult).then_inc(probs_ready, 1)
                    if b == 0 and (not isinstance(t, int) or t + 1 < NT):
                        split_x(t + 1)
                if second and not (isinstance(t, int) and t == 0):
                    pool.wait_ge(ln_step, t)
                    pool.tensor_tensor(ln[:, 1], ln[:, 0], half[:], ALU.pow).then_inc(root_made, 1)
                    for b in range(QB):
                        pool.wait_ge(normed_made, QB * (t - 1) + b + 1)
                        pool.tensor_tensor(out_sb[:, b], out_sb[:, b], gb[:, 0], ALU.mult).then_inc(gamma_made, 1)

            over_tiles(pool, body, second)

        @block.scalar
        def _(act):
            if second:
                act.wait_ge(setup_in, 48)
                act.activation(wq_hi[:], x_res[:, 0], ACT.Copy).then_inc(wq_hi_made, 1)

            def split_x(t):
                act.wait_ge(x_loaded, 16 * (t + 1))
                if not isinstance(t, int) or t >= 1:
                    act.wait_ge(acc_ready, head_turn(t - 1, HEAD - 1) + 1)
                act.activation(x_hi[:], x_in[:], ACT.Copy).then_inc(x_hi_made, 1)

            def queries(t, m):
                k = HEAD - 4 + m
                act.wait_ge(acc_ready, head_turn(t, k) + 1)
                if second:
                    wait(act, acc_read, head_reads_through(t, k) - 2 if m >= 2 else
                         (head_reads_through(t - 1, HEAD - 2 + m) if not isinstance(t, int) or t >= 1 else 0))
                    act.activation(q_full[:, m % 2], acc[:, k % 2], ACT.Relu, bias=bq[:, m:m + 1]).then_inc(relu_made, 1)
                    act.wait_ge(relu_made, 4 * t + m + 1)
                    act.activation(q_hi[:, m], q_full[:, m % 2], ACT.Copy).then_inc(acc_hi, 1)
                else:
                    act.activation(q_hi[:, m], acc[:, k % 2], ACT.Identity, bias=bq[:, m:m + 1]).then_inc(acc_hi, 1)

            def exps(t, b):
                act.wait_ge(shifted, QB * t + b + 1)
                act.activation(probs[:, b % 2], probs[:, b % 2], ACT.Exp, scale=SCALE).then_inc(exp_made, 1)

            def high_probs(t, b):
                for j in range(2):
                    n = 2 * (QB * t + b) + j
                    act.wait_ge(turned_ready, n + 1)
                    act.activation(pT_hi[:, 4 * j:4 * j + 4, b * P:(b + 1) * P], turned[:, j],
                                   ACT.Copy).then_inc(pT_hi_made, 1)

            def values(t, c):
                act.wait_ge(acc_ready, turn(t, c) + 1)
                act.activation(o_hi[:, c], acc[:, c % 2], ACT.Copy).then_inc(acc_hi, 1)

            def outputs(t, b):
                act.wait_ge(acc_ready, turn(t, 4 + b) + 1)
                if b == 0:
                    wait(act, out_stored[0], 16 * (t - 1))
                act.activation(out_sb[:, b], acc[:, b % 2], ACT.Copy).then_inc(turned_out, 1)

            def normalise(t, b):
                act.wait_ge(ln_ready, t)
                act.activation(out_sb[:, b], out_sb[:, b], ACT.Identity, bias=ln[:, 3, b:b + 1],
                               scale=ln[:, 2, b:b + 1]).then_inc(normed_made, 1)

            split_x(0)
            for m in range(4):
                queries(0, m)

            def body(t, u=None):
                first, last = isinstance(t, int) and t == 0, isinstance(t, int) and t == NT
                more = not isinstance(t, int) or t + 1 < NT
                if not last:
                    exps(t, 0)
                if not first and not second:
                    for c in range(4):
                        values(t, c)
                if not last:
                    exps(t, 1)
                if more:
                    split_x(t + 1)
                if not first and second:
                    for b in range(QB):
                        outputs(t, b)
                if not last:
                    high_probs(t, 0)
                    exps(t, 2)
                    high_probs(t, 1)
                    exps(t, 3)
                if more:
                    queries(t + 1, 0)
                    queries(t + 1, 1)
                if not last:
                    high_probs(t, 2)
                if more:
                    queries(t + 1, 2)
                    queries(t + 1, 3)
                if not first and second:
                    for b in range(QB):
                        normalise(t, b)
                if not last:
                    high_probs(t, 3)

            over_tiles(act, body, True)

        @block.vector
        def _(dve):
            if second:
                dve.wait_ge(wq_hi_made, 1)
                dve.tensor_tensor(wq_lo[:], x_res[:, 0], wq_hi[:], ALU.subtract).then_inc(wq_lo_made, 1)
                dve.wait_ge(consts_set, 1)
                dve.tensor_copy(ones_r[:], ones_f[:]).then_inc(ones_r_made, 1)
                dve.memset(neg_r[:].bitcast(F32), 0.0)

            def queries(t, m):
                k = HEAD - 4 + m
                dve.wait_ge(acc_hi, 4 * t + m + 1 if second else
                            (4 * t + m + 1 if isinstance(t, int) and t <= 1 else 8 + 8 * (t - 2) + 4 + m + 1))
                if second:
                    dve.tensor_tensor(q_lo[:, m], q_full[:, m % 2], q_hi[:, m], ALU.subtract).then_inc(acc_read, 1)
                else:
                    dve.scalar_tensor_tensor(out=q_lo[:, m], in0=acc[:, k % 2], scalar=bq[:, m:m + 1],
                                             in1=q_hi[:, m], op0=ALU.add, op1=ALU.subtract).then_inc(acc_read, 1)

            def query_mask(t, z, par):
                dve.wait_ge(acc_ready, head_turn(t, z) + 1)
                dve.tensor_scalar(q_keep[:, par, 2 * z:2 * z + 2], acc[:, z, 0:2], 0.0, None,
                                  ALU.not_equal).then_inc(acc_read, 1)

            def shift(t, b, par):
                g = QB * t + b
                dve.wait_ge(scores_ready, g + 1)
                s3 = scores[:, b % 2].rearrange("p (h s) -> p h s", s=S)
                p3 = probs[:, b % 2].rearrange("p (h s) -> p h s", s=S)
                wait(dve, turned_ready, 2 * (g - 1))
                if second and par == 0 and b == 0:
                    nth = t // 2
                    dve.tensor_tensor(p3, s3, tri[:, 0].unsqueeze(1).to_broadcast([P, HEADS, S]),
                                      ALU.mult).then_inc(causal_made, 1)
                    dve.wait_ge(causal_made, 2 * nth + 1)
                    dve.tensor_tensor(p3, p3, tri[:, 1].unsqueeze(1).to_broadcast([P, HEADS, S]),
                                      ALU.add).then_inc(causal_made, 1)
                    dve.wait_ge(causal_made, 2 * nth + 2)
                    s3 = p3
                dve.tensor_reduce(row_max[:, b % 2], s3, AX_X, ALU.max).then_inc(max_made, 1)
                dve.wait_ge(max_made, g + 1)
                dve.tensor_tensor(p3, s3, row_max[:, b % 2].unsqueeze(2).to_broadcast([P, HEADS, S]),
                                  ALU.subtract).then_inc(shifted, 1)

            def invert(t, b, par):
                g = QB * t + b
                dve.wait_ge(exp_made, g + 1)
                p3 = probs[:, b % 2].rearrange("p (h s) -> p h s", s=S)
                dve.tensor_reduce(row_sum[:, b % 2], p3, AX_X, ALU.add).then_inc(sum_made, 1)
                dve.wait_ge(sum_made, g + 1)
                wait(dve, probs_ready, g - 1)
                if second:
                    dve.reciprocal(row_inv[:, b % 2], row_sum[:, b % 2]).then_inc(inv_raw, 1)
                    dve.wait_ge(inv_raw, g + 1)
                    dve.tensor_scalar(row_inv[:, b % 2], row_inv[:, b % 2], q_keep[:, par, b:b + 1], None,
                                      ALU.mult).then_inc(inv_made, 1)
                else:
                    dve.reciprocal(row_inv[:, b % 2], row_sum[:, b % 2]).then_inc(inv_made, 1)

            def low_probs(t, b):
                for j in range(2):
                    dve.wait_ge(pT_hi_made, 2 * (QB * t + b) + j + 1)
                    dve.tensor_tensor(pT_lo[:, 4 * j:4 * j + 4, b * P:(b + 1) * P], turned[:, j],
                                      pT_hi[:, 4 * j:4 * j + 4, b * P:(b + 1) * P],
                                      ALU.subtract).then_inc(pT_lo_made, 1)

            def values(t, c, par):
                if second:
                    if c == 0:
                        dve.wait_ge(res_loaded[1 - par], 16 * ((t - 1 - (1 - par)) // 2 + 1))
                    dve.wait_ge(acc_ready, turn(t, c) + 1)
                    dve.tensor_tensor(x_res[:, 1 - par, c], acc[:, c % 2], x_res[:, 1 - par, c],
                                      ALU.add).then_inc(acc_read, 1)
                else:
                    dve.wait_ge(acc_hi, hi_reads_through(t, c + 1))
                    dve.tensor_tensor(o_lo[:, c], acc[:, c % 2], o_hi[:, c], ALU.subtract).then_inc(acc_read, 1)

            def residual(t, m, par):
                if m == 0:
                    dve.wait_ge(res_loaded[1 - par], 16 * ((t - 1 - (1 - par)) // 2 + 1))
                dve.wait_ge(acc_ready, turn(t, 4 + m) + 1)
                dve.scalar_tensor_tensor(out=x_res[:, 1 - par, m], in0=acc[:, m % 2], scalar=persist["bo"][:, m:m + 1],
                                         in1=x_res[:, 1 - par, m], op0=ALU.add, op1=ALU.add).then_inc(acc_read, 1)

            def layer_stats(t):
                for b in range(QB):
                    dve.wait_ge(turned_out, QB * (t - 1) + b + 1)
                    dve.bn_stats(stats[:, b], out_sb[:, b]).then_inc(stats_made, 1)
                dve.wait_ge(stats_made, 2 * QB * (t - 1) + QB)
                dve.memset(wait_slot[:], 0.0)
                for b in range(QB):
                    dve.bn_aggr(mean_var[:, b], stats[:, b]).then_inc(stats_made, 1)
                dve.wait_ge(stats_made, 2 * QB * t)
                dve.tensor_scalar(ln[:, 0], mean_var[:, :, 1], float(DIM) / (DIM - 1), None,
                                  ALU.mult).then_inc(ln_step, 1)

            def layer_scale(t):
                dve.wait_ge(root_made, t)
                dve.tensor_scalar(ln[:, 1], ln[:, 1], EPS, None, ALU.add).then_inc(sc_step, 1)
                dve.wait_ge(sc_step, 2 * (t - 1) + 1)
                wait(dve, normed_made, QB * (t - 1))
                dve.reciprocal(ln[:, 2], ln[:, 1]).then_inc(sc_step, 1)
                dve.wait_ge(sc_step, 2 * t)
                dve.scalar_tensor_tensor(out=ln[:, 3], in0=mean_var[:, :, 0], scalar=-1.0, in1=ln[:, 2],
                                         op0=ALU.mult, op1=ALU.mult).then_inc(ln_ready, 1)

            def layer_shift(t):
                for b in range(QB):
                    dve.wait_ge(gamma_made, QB * (t - 1) + b + 1)
                    dve.tensor_tensor(out_sb[:, b], out_sb[:, b], gb[:, 1], ALU.add).then_inc(beta_made, 1)

            if second:
                for z in range(2):
                    query_mask(0, z, 0)
            for m in range(4):
                queries(0, m)

            def body(t, u=None):
                u = t % 2 if u is None else u
                first, last = isinstance(t, int) and t == 0, isinstance(t, int) and t == NT
                more = not isinstance(t, int) or t + 1 < NT
                prev = not first
                if second and u == 0 and not last:
                    nth = t // 2
                    wait(dve, scores_ready, QB * t)
                    b0 = (t // 2) * S
                    src = persist["neg_row"][0:1, b0:b0 + S] if isinstance(t, int) else \
                        persist["neg_row"][0:1, bass.ds((t // 2) * S, S)]
                    dve.tensor_copy(neg_r[:].rearrange("p (h s) -> p h s", s=S),
                                    src.unsqueeze(1).to_broadcast([1, HEADS, S])).then_inc(neg_set, 1)
                if not last:
                    shift(t, 0, u)
                if prev:
                    values(t, 0, u)
                    values(t, 1, u)
                if not last:
                    shift(t, 1, u)
                    invert(t, 0, u)
                if prev:
                    values(t, 2, u)
                    values(t, 3, u)
                if not last:
                    invert(t, 1, u)
                if prev and not second:
                    residual(t, 0, u)
                    residual(t, 1, u)
                if not last:
                    low_probs(t, 0)
                    shift(t, 2, u)
                if prev and not second:
                    residual(t, 2, u)
                    residual(t, 3, u)
                if not last:
                    low_probs(t, 1)
                    shift(t, 3, u)
                    invert(t, 2, u)
                if prev and second:
                    layer_stats(t)
                if more and second:
                    query_mask(t + 1, 0, 1 - u)
                    query_mask(t + 1, 1, 1 - u)
                if more:
                    queries(t + 1, 0)
                    queries(t + 1, 1)
                if not last:
                    invert(t, 3, u)
                    low_probs(t, 2)
                if prev and second:
                    layer_scale(t)
                if more:
                    queries(t + 1, 2)
                    queries(t + 1, 3)
                if not last:
                    low_probs(t, 3)
                if prev and second:
                    layer_shift(t)

            over_tiles(dve, body, True)

        @block.tensor
        def _(pe):
            if second:
                pe.wait_ge(wq_lo_made, 1)
                pe.wait_ge(ones_r_made, 1)

            def query_sums(t):
                pe.wait_ge(part_made, 3 * (t + 1))
                for z in range(2):
                    if isinstance(t, int) and t == 0:
                        pass
                    else:
                        bank_free(pe, t - 1, 8 + z) if not isinstance(t, int) or t > 1 else \
                            wait(pe, acc_read, HEAD * t + z - 1)
                    for b in range(2):
                        blk = 2 * z + b
                        mm = pe.matmul(acc[:, z, b:b + 1], x_part[:, 0, blk * P:(blk + 1) * P], ones[:, 0:1],
                                       start=True, stop=True)
                    mm.then_inc(acc_ready, 1)

            def queries(t, m):
                k = HEAD - 4 + m
                if m == 0:
                    pe.wait_ge(x_lo_made, t + 1)
                if isinstance(t, int) and t <= 1:
                    wait(pe, acc_read, HEAD * t + k - 1)
                else:
                    bank_free(pe, t - 1, 8 + k)
                n = 0
                for c in range(C):
                    for w, x in ((wq_hi, x_hi), (wq_hi, x_lo), (wq_lo, x_hi)):
                        mm = pe.matmul(acc[:, k % 2], w[:, c, m * P:(m + 1) * P], x[:, c],
                                       start=(n == 0), stop=(n == 3 * C - 1))
                        n += 1
                mm.then_inc(acc_ready, 1)

            def score(t, b, par):
                g = QB * t + b
                if b == 0:
                    pe.wait_ge(acc_read, head_reads_through(t, HEAD - 1))
                    if par == 0:
                        pe.wait_ge(k_loaded, 16 * 2 * HC * (t // 2 + 1))
                        if second:
                            pe.wait_ge(neg_set, t // 2 + 1)
                wait(pe, shifted, g - 1)
                for c in range(C):
                    dst = scores[:, b % 2, c * HC * S:(c + 1) * HC * S]
                    q = slice(b * P, (b + 1) * P)
                    start = c % 2 == 0
                    if second and start:
                        half_bank = scores[:, b % 2, c * HC * S:c * HC * S + HALF]
                        pe.matmul(half_bank, ones_r[:], neg_r[:, 0:HALF], start=True, stop=False,
                                  skip_group_check=True)
                        start = False
                    pe.matmul(dst, q_hi[:, c, q], k_hl[:, 0, c], start=start, stop=False, skip_group_check=True)
                    pe.matmul(dst, q_hi[:, c, q], k_hl[:, 1, c], start=False, stop=False, skip_group_check=True)
                    mm = pe.matmul(dst, q_lo[:, c, q], k_hl[:, 0, c], start=False, stop=True, skip_group_check=True)
                mm.then_inc(scores_ready, 1)

            def turn_probs(t, b):
                g = QB * t + b
                pe.wait_ge(probs_ready, g + 1)
                for j in range(2):
                    wait(pe, pT_lo_made, 2 * g + j - 1)
                    for i in range(4):
                        pair = 4 * j + i
                        mm = pe.transpose(turned[:, j, i], probs[:, b % 2, pair * P:(pair + 1) * P], ident[:])
                    mm.then_inc(turned_ready, 1)

            def values(t, c, par):
                if c == 0:
                    pe.wait_ge(pT_lo_made, 2 * QB * t)
                    nb = (t + 1) // 2 if isinstance(t, int) else (t + par) // 2
                    pe.wait_ge(v_loaded, 16 * 8 * nb)
                bank_free(pe, t, c)
                n = 0
                for e in range(2):
                    for part, x in ((0, pT_hi), (0, pT_lo), (1, pT_hi)):
                        mm = pe.matmul(acc[:, c % 2], v_hl[:, part, c, e], x[:, 2 * c + e],
                                       start=(n == 0), stop=(n == 5))
                        n += 1
                mm.then_inc(acc_ready, 1)

            def project(t, m, par):
                if m == 0:
                    pe.wait_ge(acc_read, dve_reads_through(t, 3))
                bank_free(pe, t, 4 + m)
                n = 0
                for c in range(C):
                    for w, x in ((wo_hi, o_hi), (wo_hi, o_lo), (wo_lo, o_hi)):
                        mm = pe.matmul(acc[:, m % 2], w[:, c, m * P:(m + 1) * P], x[:, c],
                                       start=(n == 0), stop=(n == 3 * C - 1))
                        n += 1
                mm.then_inc(acc_ready, 1)

            def turn_out(t, b, par):
                if b == 0:
                    pe.wait_ge(acc_read, dve_reads_through(t, 3))
                bank_free(pe, t, 4 + b)
                for c in range(C):
                    mm = pe.transpose(acc[:, b % 2, c * P:(c + 1) * P], x_res[:, 1 - par, c, b * P:(b + 1) * P], ident[:])
                mm.then_inc(acc_ready, 1)

            finish = turn_out if second else project
            if second:
                query_sums(0)
            for m in range(4):
                queries(0, m)

            def body(t, u=None):
                u = t % 2 if u is None else u
                first, last = isinstance(t, int) and t == 0, isinstance(t, int) and t == NT
                more = not isinstance(t, int) or t + 1 < NT
                if not last:
                    score(t, 0, u)
                if not first:
                    values(t, 0, u)
                    values(t, 1, u)
                if not last:
                    score(t, 1, u)
                if not first:
                    values(t, 2, u)
                    values(t, 3, u)
                    finish(t, 0, u)
                    finish(t, 1, u)
                if not last:
                    turn_probs(t, 0)
                    score(t, 2, u)
                if not first:
                    finish(t, 2, u)
                    finish(t, 3, u)
                if not last:
                    turn_probs(t, 1)
                    score(t, 3, u)
                if more:
                    if second:
                        query_sums(t + 1)
                    queries(t + 1, 0)
                    queries(t + 1, 1)
                if not last:
                    turn_probs(t, 2)
                if more:
                    queries(t + 1, 2)
                    queries(t + 1, 3)
                if not last:
                    turn_probs(t, 3)

            over_tiles(pe, body, True)


def build_mlp(nc, io, persist, scratch):
    x_dram = scratch["x1"].rearrange("(c p) n -> p c n", p=P)
    y_dram = scratch["x2"].rearrange("(c p) n -> p c n", p=P)
    RING = 3
    LAG = 2

    with ExitStack() as ctx:
        def sb(name, shape, dt=F32):
            return ctx.enter_context(nc.sbuf_tensor(f"mlp_{name}", shape, dt))

        def sem(name):
            return ctx.enter_context(nc.semaphore(f"mlp_{name}"))

        w1_hi = sb("w1_hi", [P, J, C, P], F32R)
        w1_lo = sb("w1_lo", [P, J, C, P], F32R)
        w2_hi = sb("w2_hi", [P, J, DIM], F32R)
        w2_lo = sb("w2_lo", [P, J, DIM], F32R)
        w_raw = sb("w_raw", [P, 2, 2, DIM])
        x = sb("x", [P, 2, C, N])
        x_hi = sb("x_hi", [P, 2, C, N], F32R)
        x_lo = sb("x_lo", [P, 2, C, N], F32R)
        g_full = sb("g_full", [P, 2, N])
        g_hi = sb("g_hi", [P, 2, N], F32R)
        g_lo = sb("g_lo", [P, 2, N], F32R)
        hid = ctx.enter_context(nc.psum_tensor("mlp_hid", [P, 4, N], F32))
        acc = ctx.enter_context(nc.psum_tensor("mlp_acc", [P, C, N], F32))

        w_loaded = [sem("w_loaded0"), sem("w_loaded1")]
        w_hi_made = sem("w_hi_made")
        w_lo_made = sem("w_lo_made")
        x_loaded = [sem("x_loaded0"), sem("x_loaded1")]
        x_hi_made = sem("x_hi_made")
        x_lo_made = sem("x_lo_made")
        hid_ready = sem("hid_ready")
        gelu_made = sem("gelu_made")
        g_hi_made = sem("g_hi_made")
        g_lo_made = sem("g_lo_made")
        out_part = sem("out_part")
        out_ready = sem("out_ready")
        out_read = sem("out_read")
        stored = [sem("stored0"), sem("stored1")]
        b1, b2 = persist["b1"], persist["b2"]

        block = ctx.enter_context(nc.Block())

        @block.sync
        def _(sp):
            def load_x(t, u):
                cols = bass.ds(t * N, N) if not isinstance(t, int) else slice(t * N, (t + 1) * N)
                sp.dma_start(x[:, u], x_dram[:, :, cols]).then_inc(x_loaded[u], 16)

            load_x(0, 0)
            w1v = io["w1"].rearrange("(c p) (j n) -> j p c n", p=P, n=P)
            for j in range(J):
                if j >= 2:
                    sp.wait_ge(w_lo_made, j - 1)
                if j == 4:
                    load_x(1, 1)
                sp.dma_start(w_raw[:, j % 2, 0].rearrange("p (c n) -> p c n", c=C), w1v[j]).then_inc(w_loaded[j % 2], 16)
                sp.dma_start(w_raw[:, j % 2, 1], io["w2"][j * P:(j + 1) * P, :]).then_inc(w_loaded[j % 2], 16)

            def body(t, u=None):
                u = t % 2 if u is None else u
                if not isinstance(t, int) or 1 <= t < NT - 1:
                    sp.wait_ge(stored[1 - u], 16 * ((t - 1 - (1 - u)) // 2 + 1))
                    load_x(t + 1, 1 - u)
                sp.wait_ge(out_read, C * (t + 1))
                cols = bass.ds(t * N, N) if not isinstance(t, int) else slice(t * N, (t + 1) * N)
                sp.dma_start(y_dram[:, :, cols], x[:, u]).then_inc(stored[u], 16)

            over_tiles(sp, body, False)
            for u in range(2):
                sp.wait_ge(stored[u], 16 * NT // 2)

        def split_x_hi(act, t, u):
            act.wait_ge(x_loaded[u], 16 * ((t - u) // 2 + 1))
            if not isinstance(t, int) or t >= 2:
                act.wait_ge(hid_ready, J * (t - 1))
            act.activation(x_hi[:, u], x[:, u], ACT.Copy).then_inc(x_hi_made, 1)

        @block.scalar
        def _(act):
            split_x_hi(act, 0, 0)

            def body(t, u=None):
                u = t % 2 if u is None else u
                for j in range(J):
                    if isinstance(t, int) and t == 0:
                        act.wait_ge(w_loaded[j % 2], 32 * (j // 2 + 1))
                        act.activation(w1_hi[:, j].rearrange("p c n -> p (c n)"), w_raw[:, j % 2, 0],
                                       ACT.Copy).then_inc(w_hi_made, 1)
                        act.activation(w2_hi[:, j], w_raw[:, j % 2, 1], ACT.Copy).then_inc(w_hi_made, 1)
                        if j >= LAG:
                            gelu(t, j - LAG)
                    else:
                        gelu(t, j)
                    if j == 8 and (not isinstance(t, int) or t + 1 < NT):
                        split_x_hi(act, t + 1, 1 - u)
                if isinstance(t, int) and t == 0:
                    for j in range(J - LAG, J):
                        gelu(t, j)

            def gelu(t, j):
                n = J * t + j
                act.wait_ge(hid_ready, n + 1)
                wait(act, g_lo_made, n - 1)
                act.activation(g_full[:, j % 2], hid[:, j % 4], ACT.Gelu_apprx_tanh,
                               bias=b1[:, j:j + 1]).then_inc(gelu_made, 1)

            over_tiles(act, body, False)

        @block.vector
        def _(dve):
            def split_x_lo(t, u):
                dve.wait_ge(x_hi_made, t + 1)
                dve.tensor_tensor(x_lo[:, u], x[:, u], x_hi[:, u], ALU.subtract).then_inc(x_lo_made, 1)

            def split_hidden(t, j):
                n = J * t + j
                dve.wait_ge(gelu_made, n + 1)
                if j == 1:
                    wait(dve, out_ready, C * t)
                else:
                    wait(dve, out_part, (J - 1) * t + (j - 1 if j else 0))
                dve.tensor_copy(g_hi[:, j % 2], g_full[:, j % 2]).then_inc(g_hi_made, 1)
                dve.wait_ge(g_hi_made, n + 1)
                dve.tensor_tensor(g_lo[:, j % 2], g_full[:, j % 2], g_hi[:, j % 2], ALU.subtract).then_inc(g_lo_made, 1)

            split_x_lo(0, 0)

            def body(t, u=None):
                u = t % 2 if u is None else u
                for j in range(J):
                    if isinstance(t, int) and t == 0:
                        dve.wait_ge(w_hi_made, 2 * j + 2)
                        dve.tensor_tensor(w1_lo[:, j].rearrange("p c n -> p (c n)"), w_raw[:, j % 2, 0],
                                          w1_hi[:, j].rearrange("p c n -> p (c n)"), ALU.subtract)
                        dve.tensor_tensor(w2_lo[:, j], w_raw[:, j % 2, 1], w2_hi[:, j], ALU.subtract).then_inc(w_lo_made, 1)
                        if j >= LAG:
                            split_hidden(t, j - LAG)
                    else:
                        split_hidden(t, j)
                    if j == 8 and (not isinstance(t, int) or t + 1 < NT):
                        split_x_lo(t + 1, 1 - u)
                if isinstance(t, int) and t == 0:
                    for j in range(J - LAG, J):
                        split_hidden(t, j)
                for m in range(C):
                    dve.wait_ge(out_ready, C * t + m + 1)
                    dve.scalar_tensor_tensor(out=x[:, u, m], in0=acc[:, m], scalar=b2[:, m:m + 1], in1=x[:, u, m],
                                             op0=ALU.add, op1=ALU.add).then_inc(out_read, 1)

            over_tiles(dve, body, False)

        @block.tensor
        def _(pe):
            def first(t, j, u):
                if j == 0:
                    pe.wait_ge(x_lo_made, t + 1)
                if isinstance(t, int) and t == 0:
                    pe.wait_ge(w_lo_made, j + 1)
                wait(pe, gelu_made, J * t + j - 3)
                n = 0
                for c in range(C):
                    for w, xs in ((w1_hi, x_hi), (w1_hi, x_lo), (w1_lo, x_hi)):
                        mm = pe.matmul(hid[:, j % 4], w[:, j, c], xs[:, u, c], start=(n == 0), stop=(n == 3 * C - 1))
                        n += 1
                mm.then_inc(hid_ready, 1)

            def then(t, j, u):
                pe.wait_ge(g_lo_made, J * t + j + 1)
                for m in range(C):
                    if j == 0:
                        wait(pe, out_read, C * (t - 1) + m + 1)
                    for n, (w, g) in enumerate(((w2_hi, g_hi), (w2_hi, g_lo), (w2_lo, g_hi))):
                        mm = pe.matmul(acc[:, m], w[:, j, m * P:(m + 1) * P], g[:, j % 2],
                                       start=(j == 0 and n == 0), stop=(j == J - 1 and n == 2))
                    if j == J - 1:
                        mm.then_inc(out_ready, 1)
                    elif m == C - 1:
                        mm.then_inc(out_part, 1)

            def body(t, u=None):
                u = t % 2 if u is None else u
                for j in range(J + LAG):
                    if j < J:
                        first(t, j, u)
                    if j >= LAG:
                        then(t, j - LAG, u)

            over_tiles(pe, body, False)


def build(nc, io):
    with ExitStack() as ctx:
        def sb(name, shape, dt=F32):
            return ctx.enter_context(nc.sbuf_tensor(name, shape, dt))

        bias = sb("bias", [P, 6 * C + J])
        persist = {"bias": bias, "ident": sb("ident", [P, P]), "zeros": sb("zeros", [P, 1]),
                   "neg_row": sb("neg_row", [1, BS])}
        cols = [bias[:, C * i:C * (i + 1)] for i in range(6)]
        persist["bq"] = [cols[0], cols[1]]
        persist["bk"] = [cols[2], cols[3]]
        persist["bo"], persist["b2"] = cols[4], cols[5]
        persist["b1"] = bias[:, 6 * C:6 * C + J]
        scratch = {
            "k": nc.dram_tensor("k_scratch", [2, 2, C, P, BS], F32, kind="Internal").ap(),
            "v": nc.dram_tensor("v_scratch", [2, 2, BS, DIM], F32, kind="Internal").ap(),
            "x1": nc.dram_tensor("x1_scratch", [DIM, B * TOK], F32, kind="Internal").ap(),
            "x2": nc.dram_tensor("x2_scratch", [DIM, B * TOK], F32, kind="Internal").ap(),
        }
        with ExitStack() as early:
            for name in ("wq_hi", "wq_lo", "wo_hi", "wo_lo"):
                persist[name] = early.enter_context(nc.sbuf_tensor(name, [P, C, DIM], F32R))
            build_keys(nc, io, persist, scratch)
            build_attention(nc, io, persist, scratch, 0)
        build_mlp(nc, io, persist, scratch)
        build_attention(nc, io, persist, scratch, 1)


def kernel(x, ctx_1024, L0_xattn_Wq, L0_xattn_bq, L0_xattn_Wk, L0_xattn_bk, L0_xattn_Wv, L0_xattn_bv,
           L0_xattn_Wo, L0_xattn_bo, L0_xattn_W1, L0_xattn_b1, L0_xattn_W2, L0_xattn_b2,
           L1_xattn_Wq, L1_xattn_bq, L1_xattn_Wk, L1_xattn_bk, L1_xattn_Wv, L1_xattn_bv,
           L1_xattn_gamma, L1_xattn_beta):
    import numpy as np
    import concourse.bacc as bacc
    from concourse.bass_utils import run_bass_kernel_spmd

    def by_chunk(v):
        return np.asarray(v).reshape(-1, P).T

    def rows(*vs):
        return np.ascontiguousarray(np.broadcast_to(np.stack([np.asarray(v) for v in vs])[None], (P, len(vs), DIM)))

    allowed = (np.arange(P)[:, None] >= np.arange(S)[None, :]).astype(np.float32)
    arrays = {
        "xT": np.asarray(x).reshape(B * TOK, DIM).T,
        "ctxT": np.asarray(ctx_1024).reshape(BS, DIM).T,
        "wq0": L0_xattn_Wq, "wk0": L0_xattn_Wk, "wv0": L0_xattn_Wv, "wo0": L0_xattn_Wo,
        "w1": L0_xattn_W1, "w2": L0_xattn_W2,
        "wq1": np.asarray(L1_xattn_Wq).T, "wk1": np.asarray(L1_xattn_Wk).T, "wv1": np.asarray(L1_xattn_Wv).T,
        "bias": np.concatenate([by_chunk(v) for v in (L0_xattn_bq, L1_xattn_bq, L0_xattn_bk, L1_xattn_bk,
                                                      L0_xattn_bo, L0_xattn_b2, L0_xattn_b1)], axis=1),
        "bv": rows(L0_xattn_bv, L1_xattn_bv),
        "gb": rows(L1_xattn_gamma, L1_xattn_beta),
        "ident": np.eye(P, dtype=np.float32),
        "tri": np.stack([allowed, np.where(allowed > 0, 0.0, NEG).astype(np.float32)], axis=1),
    }
    arrays = {f"in_{k}": np.ascontiguousarray(v) for k, v in arrays.items()}
    nc = bacc.Bacc("TRN2", target_bir_lowering=False, num_devices=1)
    io = {k[3:]: nc.dram_tensor(k, a.shape, mybir.dt.from_np(a.dtype), kind="ExternalInput").ap()
          for k, a in arrays.items()}
    io["out"] = nc.dram_tensor("out", (B * TOK, DIM), F32, kind="ExternalOutput").ap()
    build(nc, io)
    r = run_bass_kernel_spmd(nc, [arrays], core_ids=[0])
    return r.results[0]["out"].reshape(B, TOK, DIM)
```

```python
from contextlib import ExitStack

import concourse.bass as bass
from concourse import mybir

F32 = mybir.dt.float32
F32R = mybir.dt.float32r
ALU = mybir.AluOpType
ACT = mybir.ActivationFunctionType
AX_X = mybir.AxisListType.X

P = 128
DIM = 512
C = DIM // P
HEADS = 16
HD = DIM // HEADS
FF = 4 * DIM
J = FF // P
B = 8
S = 64
TOK = 1024
N = 512
TPB = TOK // N
NT = B * TPB
QB = N // P
HC = P // HD
PAIRS = HEADS // 2
BS = B * S
HALF = HEADS * S // 2
SCALE = 1.0 / float(HD) ** 0.5
NEG = -4294967295.0 * float(HD) ** 0.5
EPS = 1e-8


def wait(eng, sem, value):
    if not isinstance(value, int) or value > 0:
        eng.wait_ge(sem, value)


def over_tiles(eng, body, last_step, peeled=1):
    for t in range(peeled * TPB):
        body(t)
    with eng.Fori(peeled, B - 1) as b:
        for u in range(TPB):
            body(b * TPB + u, u)
    for t in range(NT - TPB, NT):
        body(t)
    if last_step:
        body(NT)


def build_keys(nc, io, persist, scratch):
    with ExitStack() as ctx:
        def sb(name, shape, dt=F32):
            return ctx.enter_context(nc.sbuf_tensor(name, shape, dt))

        def sem(name):
            return ctx.enter_context(nc.semaphore(name))

        ctx_raw = sb("kv_ctx_raw", [P, C, BS])
        ctx_hi = sb("kv_ctx_hi", [P, C, BS], F32R)
        ctx_lo = sb("kv_ctx_lo", [P, C, BS], F32R)
        w_raw = sb("kv_w_raw", [P, 2, C, DIM])
        w_hi = sb("kv_w_hi", [P, 2, C, DIM], F32R)
        w_lo = sb("kv_w_lo", [P, 2, C, DIM], F32R)
        bv = sb("kv_bv", [P, 2, DIM])
        ones = sb("kv_ones", [P, P])
        keep = sb("kv_keep", [P, BS])
        neg_row = sb("kv_neg_row", [1, BS])
        full = sb("kv_full", [P, 2, DIM])
        out_hi = sb("kv_out_hi", [P, 2, DIM], F32R)
        out_lo = sb("kv_out_lo", [P, 2, DIM], F32R)
        acc = ctx.enter_context(nc.psum_tensor("kv_acc", [P, 4, DIM], F32))

        small_in = sem("kv_small_in")
        ctx_in = sem("kv_ctx_in")
        w_in = [sem("kv_w_in0"), sem("kv_w_in1")]
        ones_set = sem("kv_ones_set")
        ctx_split_hi = sem("kv_ctx_split_hi")
        ctx_split_lo = sem("kv_ctx_split_lo")
        w_split_hi = sem("kv_w_split_hi")
        w_split_lo = sem("kv_w_split_lo")
        kept_split_lo = sem("kv_kept_split_lo")
        x_in_loaded = sem("kv_x_in_loaded")
        rows_summed = sem("kv_rows_summed")
        keep_made = sem("kv_keep_made")
        neg_made = sem("kv_neg_made")
        neg_stored = sem("kv_neg_stored")
        group_ready = sem("kv_group_ready")
        group_read = sem("kv_group_read")
        masked = sem("kv_masked")
        hi_made = sem("kv_hi_made")
        lo_made = sem("kv_lo_made")
        stored = [sem("kv_stored0"), sem("kv_stored1")]
        bk = persist["bk"]
        weights = [io["wk0"], io["wv0"], io["wk1"], io["wv1"], io["wq0"], io["wo0"]]
        NW = len(weights)
        KV = 4
        GROUPS = KV * C

        block = ctx.enter_context(nc.Block())

        @block.sync
        def _(sp):
            sp.dma_start(ctx_raw[:], io["ctxT"].rearrange("(c p) n -> p c n", p=P)).then_inc(ctx_in, 16)
            sp.dma_start(persist["bias"][:], io["bias"]).then_inc(small_in, 16)
            sp.dma_start(bv[:], io["bv"]).then_inc(small_in, 16)
            sp.dma_start(persist["ident"][:], io["ident"]).then_inc(small_in, 16)

            def load_weight(i):
                sp.dma_start(w_raw[:, i % 2], weights[i].rearrange("(c p) n -> p c n", p=P)).then_inc(w_in[i % 2], 16)

            load_weight(0)
            load_weight(1)
            sp.wait_ge(neg_made, 1)
            sp.dma_start(scratch["neg"], neg_row[:]).then_inc(neg_stored, 16)
            for g in range(GROUPS):
                i, m = g // C, g % C
                if m == 0:
                    sp.wait_ge(w_split_lo, i + 1)
                    load_weight(i + 2)
                layer = i // 2
                sp.wait_ge(lo_made, g + 1)
                for part, src in ((0, out_hi), (1, out_lo)):
                    if i % 2 == 0:
                        dst = scratch["k"][layer, part, m]
                    else:
                        dst = scratch["v"][layer, part, m * P:(m + 1) * P, :]
                    sp.dma_start(dst, src[:, g % 2].bitcast(F32)).then_inc(stored[g % 2], 16)
            sp.dma_start(persist["x_in"][:], io["xT"].rearrange("(c p) n -> p c n", p=P)[:, :, :N]).then_inc(x_in_loaded, 16)
            for s in range(2):
                sp.wait_ge(stored[s], 16 * 2 * GROUPS // 2)
            sp.wait_ge(x_in_loaded, 16)
            sp.wait_ge(small_in, 48)
            sp.wait_ge(neg_stored, 16)

        @block.scalar
        def _(act):
            act.wait_ge(ctx_in, 16)
            act.activation(ctx_hi[:], ctx_raw[:], ACT.Copy).then_inc(ctx_split_hi, 1)
            for i in range(NW):
                act.wait_ge(w_in[i % 2], 16 * (i // 2 + 1))
                if i < KV:
                    if i >= 2:
                        act.wait_ge(group_ready, C * (i - 1))
                    dst = w_hi[:, i % 2]
                else:
                    dst = persist["wq_hi"][:] if i == KV else persist["wo_hi"][:]
                act.activation(dst, w_raw[:, i % 2], ACT.Copy).then_inc(w_split_hi, 1)

        @block.gpsimd
        def _(pool):
            pool.memset(ones[:], 1.0).then_inc(ones_set, 1)
            for i, name in ((KV, "wq"), (KV + 1, "wo")):
                pool.wait_ge(w_split_hi, i + 1)
                pool.tensor_tensor(persist[name + "_lo"][:], w_raw[:, i % 2], persist[name + "_hi"][:],
                                   ALU.subtract).then_inc(kept_split_lo, 1)

        @block.vector
        def _(dve):
            dve.wait_ge(ctx_split_hi, 1)
            dve.tensor_tensor(ctx_lo[:], ctx_raw[:], ctx_hi[:], ALU.subtract).then_inc(ctx_split_lo, 1)

            def split_weight(i):
                dve.wait_ge(w_split_hi, i + 1)
                if i >= 2:
                    dve.wait_ge(group_ready, C * (i - 1))
                dve.tensor_tensor(w_lo[:, i % 2], w_raw[:, i % 2], w_hi[:, i % 2], ALU.subtract).then_inc(w_split_lo, 1)

            split_weight(0)
            split_weight(1)
            dve.wait_ge(rows_summed, 1)
            dve.tensor_scalar(keep[:], acc[:, 3], 0.0, None, ALU.not_equal).then_inc(keep_made, 1)
            dve.wait_ge(keep_made, 1)
            dve.tensor_scalar(neg_row[:], keep[0:1, :], -NEG, NEG, ALU.mult, ALU.add).then_inc(neg_made, 1)
            dve.wait_ge(small_in, 48)
            for g in range(GROUPS):
                i, m = g // C, g % C
                slot = g % 2
                if g % C == 0 and g:
                    if i + 1 < KV:
                        split_weight(i + 1)
                dve.wait_ge(group_ready, g + 1)
                a = acc[:, slot]
                f = full[:, slot]
                if i % 2 == 0:
                    dve.tensor_scalar(f, a, bk[i // 2][:, m:m + 1], 0.0 if i else None,
                                      ALU.add, ALU.max if i else ALU.bypass).then_inc(group_read, 1)
                else:
                    dve.tensor_tensor(f, a, bv[:, i // 2, :], ALU.add).then_inc(group_read, 1)
                dve.wait_ge(group_read, g + 1)
                if i == 2:
                    dve.tensor_tensor(f, f, keep[:], ALU.mult).then_inc(masked, 1)
                    dve.wait_ge(masked, m + 1)
                if i == 3:
                    dve.tensor_scalar(f, f, 0.0, None, ALU.max).then_inc(masked, 1)
                    dve.wait_ge(masked, C + m + 1)
                if g >= 2:
                    dve.wait_ge(stored[slot], 32 * (g // 2))
                dve.tensor_copy(out_hi[:, slot], f).then_inc(hi_made, 1)
                dve.wait_ge(hi_made, g + 1)
                dve.tensor_tensor(out_lo[:, slot], f, out_hi[:, slot], ALU.subtract).then_inc(lo_made, 1)

        @block.tensor
        def _(pe):
            pe.wait_ge(ctx_in, 16)
            pe.wait_ge(ones_set, 1)
            for c in range(C):
                mm = pe.matmul(acc[:, 3], ones[:], ctx_raw[:, c], start=(c == 0), stop=(c == C - 1))
            mm.then_inc(rows_summed, 1)
            pe.wait_ge(ctx_split_lo, 1)
            for g in range(GROUPS):
                i, m = g // C, g % C
                if m == 0:
                    pe.wait_ge(w_split_lo, i + 1)
                if g >= 2:
                    pe.wait_ge(group_read, g - 1)
                n = 0
                for c in range(C):
                    for xw in ((w_hi, ctx_hi), (w_hi, ctx_lo), (w_lo, ctx_hi)):
                        w, x = xw[0][:, i % 2, c], xw[1][:, c]
                        if i % 2 == 0:
                            mm = pe.matmul(acc[:, g % 2], w[:, m * P:(m + 1) * P], x, start=(n == 0), stop=(n == 11))
                        else:
                            mm = pe.matmul(acc[:, g % 2], x[:, m * P:(m + 1) * P], w, start=(n == 0), stop=(n == 11))
                        n += 1
                mm.then_inc(group_ready, 1)


def build_attention(nc, io, persist, scratch, layer):
    second = layer == 1
    res_dram = (scratch["x2"] if second else io["xT"]).rearrange("(c p) n -> p c n", p=P)
    y_dram = io["out"].rearrange("(t b p) n -> t p b n", b=QB, p=P) if second else \
        scratch["x1"].rearrange("(c p) n -> p c n", p=P)

    READERS = "VVVV" + ("SSSS" + "VV" + "SSSS" if second else "VVVV" + "VVVV")
    USES = len(READERS)
    HEAD = USES - 8
    LOADS_K = 2 * HC + second
    LOADS_V = 8
    SLOTS = 2 if second else 1

    with ExitStack() as ctx:
        def sb(name, shape, dt=F32):
            return ctx.enter_context(nc.sbuf_tensor(f"at{layer}_{name}", shape, dt))

        def sem(name):
            return ctx.enter_context(nc.semaphore(f"at{layer}_{name}"))

        x_hi = sb("x_hi", [P, SLOTS, C, N], F32R)
        x_lo = sb("x_lo", [P, SLOTS, C, N], F32R)
        q_hi = sb("q_hi", [P, SLOTS, C, N], F32R)
        q_lo = sb("q_lo", [P, SLOTS, C, N], F32R)
        probs = sb("probs", [P, 2, HEADS * S])
        pT_hi = sb("pT_hi", [P, PAIRS, N], F32R)
        pT_lo = sb("pT_lo", [P, PAIRS, N], F32R)
        x_res = sb("x_res", [P, 2, C, N])
        k_hl = sb("k_hl", [P, 2, C, HC * S], F32R)
        v_hl = sb("v_hl", [P, 2, C, 2, P], F32R)
        row_max = sb("row_max", [P, 2, HEADS])
        row_sum = sb("row_sum", [P, 2, HEADS])
        row_inv = sb("row_inv", [P, 2, HEADS])
        acc = ctx.enter_context(nc.psum_tensor(f"at{layer}_acc", [P, 2, N], F32))
        scores = ctx.enter_context(nc.psum_tensor(f"at{layer}_scores", [P, 2, 2 * HALF], F32))
        turned = ctx.enter_context(nc.psum_tensor(f"at{layer}_turned", [P, 2, 4, P], F32))
        ident = persist["ident"]
        bq = persist["bq"][layer]
        if second:
            wq_hi = sb("wq_hi", [P, C, DIM], F32R)
            wq_lo = sb("wq_lo", [P, C, DIM], F32R)
            wq_raw = persist["raw"][:].rearrange("p a b n -> p (a b) n")
            q_full = sb("q_full", [P, 2, N])
            x_sum = sb("x_sum", [P, 2, N])
            q_keep = sb("q_keep", [P, 2, QB])
            ones = sb("ones", [P, 2])
            ones_f = sb("ones_f", [1, P])
            ones_r = sb("ones_r", [1, P], F32R)
            neg_r = sb("neg_r", [1, S], F32R)
            tri = sb("tri", [P, 2, S])
            gb = sb("gb", [P, 2, DIM])
            stats = sb("stats", [P, QB, 6])
            wait_slot = sb("wait_slot", [P, 1])
            mean_var = sb("mean_var", [P, QB, 2])
            ln = sb("ln", [P, 4, QB])
            half = sb("half", [P, QB])
            out_sb = sb("out_sb", [P, 2, QB, DIM])
        else:
            x_in = persist["x_in"]
            wq_hi, wq_lo = persist["wq_hi"], persist["wq_lo"]
            wo_hi, wo_lo = persist["wo_hi"], persist["wo_lo"]
            o_hi = sb("o_hi", [P, C, N], F32R)
            o_lo = sb("o_lo", [P, C, N], F32R)

        x_loaded = [sem("x_loaded0"), sem("x_loaded1")]
        res_loaded = [sem("res_loaded0"), sem("res_loaded1")]
        k_loaded = sem("k_loaded")
        v_loaded = sem("v_loaded")
        out_stored = [sem("out_stored0"), sem("out_stored1")]
        kv_zeroed = sem("kv_zeroed")
        acc_ready = sem("acc_ready")
        acc_read_v = sem("acc_read_v")
        acc_read_s = sem("acc_read_s")
        scores_ready = sem("scores_ready")
        max_made = sem("max_made")
        shifted = sem("shifted")
        exp_made = sem("exp_made")
        sum_made = sem("sum_made")
        inv_made = sem("inv_made")
        probs_ready = sem("probs_ready")
        turned_ready = sem("turned_ready")
        pT_hi_made = sem("pT_hi_made")
        pT_lo_made = sem("pT_lo_made")
        q_hi_made = sem("q_hi_made")
        if second:
            setup_in = sem("setup_in")
            consts_set = sem("consts_set")
            wq_hi_made = sem("wq_hi_made")
            wq_lo_made = sem("wq_lo_made")
            ones_r_made = sem("ones_r_made")
            q_lo_made = sem("q_lo_made")
            causal_made = sem("causal_made")
            inv_raw = sem("inv_raw")
            stats_made = sem("stats_made")
            var_made = sem("var_made")
            root_made = sem("root_made")
            scale_step = sem("scale_step")
            ln_ready = sem("ln_ready")
            normed_made = sem("normed_made")
            gamma_made = sem("gamma_made")
            beta_made = sem("beta_made")
        else:
            mlp_loaded = sem("mlp_loaded")
            x_hi_made = sem("x_hi_made")
            x_lo_made = sem("x_lo_made")
            o_hi_made = sem("o_hi_made")

        def fixed(t):
            return isinstance(t, int)

        def absent(t, turns):
            return turns if fixed(t) and t == NT else 0

        def turns_through(t, k):
            return 2 * HEAD + USES * (t - 1) + k + 1 - absent(t, HEAD)

        def head_through(t, k):
            return HEAD * t + k + 1 if fixed(t) and t <= 1 else turns_through(t - 1, 8 + k)

        def reads_through(who, t, k):
            head = READERS[8:].count(who)
            return 2 * head + READERS.count(who) * (t - 1) + READERS[:k + 1].count(who) - absent(t, head)

        def head_reads_through(who, t, k):
            if fixed(t) and t <= 1:
                return READERS[8:].count(who) * t + READERS[8:8 + k + 1].count(who)
            return reads_through(who, t - 1, 8 + k)

        def ended(eng, t, k):
            who = READERS[k]
            wait(eng, acc_read_v if who == "V" else acc_read_s, reads_through(who, t, k))

        def head_ended(eng, t, k):
            who = READERS[8 + k]
            wait(eng, acc_read_v if who == "V" else acc_read_s, head_reads_through(who, t, k))

        def bank_free(pe, t, k):
            if k >= 2:
                ended(pe, t, k - 2)
            elif absent(t, 1):
                ended(pe, t - 1, 6 + k)
            else:
                head_ended(pe, t, HEAD + k - 2)

        def head_bank_free(pe, t, k):
            if k >= 2:
                head_ended(pe, t, k - 2)
            elif fixed(t) and t <= 1:
                if t == 1:
                    head_ended(pe, 0, HEAD + k - 2)
            else:
                ended(pe, t - 1, 6 + k)

        def columns(t):
            return slice(t * N, (t + 1) * N) if fixed(t) else bass.ds(t * N, N)

        def loads(t, u):
            return 16 * ((t - u) // 2 + 1)

        def low_queries_made(eng, t, m):
            if second:
                eng.wait_ge(q_lo_made, 4 * t + m + 1)
            else:
                head_ended(eng, t, m)

        block = ctx.enter_context(nc.Block())

        @block.sync
        def _(sp):
            def load_x(t, u):
                if second:
                    for dst, src in ((x_hi[:, u].bitcast(F32), scratch["x2_hi"]), (x_lo[:, u].bitcast(F32), scratch["x2_lo"])):
                        sp.dma_start(dst, src.rearrange("(c p) n -> p c n", p=P)[:, :, columns(t)]).then_inc(x_loaded[u], 16)
                    sp.dma_start(x_sum[:, u], scratch["x2_sum"][:, columns(t)]).then_inc(x_loaded[u], 16)
                else:
                    sp.dma_start(x_in[:], res_dram[:, :, columns(t)]).then_inc(x_loaded[0], 16)

            def load_k(b):
                src = scratch["k"][layer].rearrange("l c p (b s) -> b p l c s", s=S)[b]
                for h in range(HC):
                    for part in range(2):
                        sp.dma_start(k_hl[h * HD:(h + 1) * HD, part, :, h * S:(h + 1) * S].bitcast(F32),
                                     src[h * HD:(h + 1) * HD, part]).then_inc(k_loaded, 16)
                if second:
                    row = scratch["neg"].rearrange("a (b s) -> b a s", s=S)[b]
                    sp.dma_start(neg_r[:].bitcast(F32), row).then_inc(k_loaded, 16)

            def load_v(b):
                src = scratch["v"][layer].rearrange("l (b s) (c e g d) -> b e g s l c d", s=S, e=2, g=2, d=HD)[b]
                for e in range(2):
                    for g in range(2):
                        for part in range(2):
                            sp.dma_start(v_hl[g * S:(g + 1) * S, part, :, e,
                                              (2 * e + g) * HD:(2 * e + g + 1) * HD].bitcast(F32),
                                         src[e, g][:, part]).then_inc(v_loaded, 16)

            def load_residual(t, u):
                sp.dma_start(x_res[:, u], res_dram[:, :, columns(t)]).then_inc(res_loaded[u], 16)

            def store(t, u):
                if second:
                    sp.wait_ge(beta_made, QB * (t + 1))
                    sp.dma_start(y_dram[t], out_sb[:, u]).then_inc(out_stored[u], 16)
                else:
                    ended(sp, t + 1, 7)
                    sp.dma_start(y_dram[:, :, columns(t)], x_res[:, u]).then_inc(out_stored[u], 16)

            if second:
                load_x(0, 0)
                sp.dma_start(tri[:], io["tri"]).then_inc(setup_in, 16)
                sp.dma_start(gb[:], io["gb"]).then_inc(setup_in, 16)
            sp.wait_ge(kv_zeroed, 1)

            def body(t, u=None):
                u = t % 2 if u is None else u
                last, more = fixed(t) and t == NT, not fixed(t) or t + 1 < NT
                if u == 0 and not last:
                    wait(sp, scores_ready, QB * t)
                    load_k(t // 2)
                if second and fixed(t) and t == 0:
                    load_x(1, 1)
                if second and (not fixed(t) or t >= 3):
                    store(t - 3, 1 - u)
                if more and not second:
                    sp.wait_ge(x_lo_made, t + 1)
                    load_x(t + 1, 1 - u)
                if second and (not fixed(t) or 1 <= t < NT - 1):
                    sp.wait_ge(acc_ready, head_through(t - 1, HEAD - 1))
                    load_x(t + 1, 1 - u)
                if not last:
                    if not fixed(t) or t >= 2:
                        if second:
                            sp.wait_ge(acc_ready, turns_through(t - 1, 7))
                        else:
                            sp.wait_ge(out_stored[u], 16 * ((t - u) // 2))
                    load_residual(t, u)
                if u == 0 and not last:
                    if not fixed(t) or t > 0:
                        sp.wait_ge(acc_ready, turns_through(t, 3))
                    load_v(t // 2)
                if not second and not (fixed(t) and t == 0):
                    store(t - 1, 1 - u)
                if not second and fixed(t) and t == NT - 1:
                    for j in range(2):
                        load_mlp_weights(sp, io, persist["raw"], j, mlp_loaded)

            over_tiles(sp, body, True, 2 if second else 1)
            if not second:
                sp.wait_ge(mlp_loaded, 64)
            if second:
                store(NT - 2, (NT - 2) % 2)
                store(NT - 1, (NT - 1) % 2)
            for u in range(2):
                sp.wait_ge(out_stored[u], 16 * NT // 2)

        @block.gpsimd
        def _(pool):
            if second:
                pool.memset(ones[:], 1.0)
                pool.memset(ones_f[:], 1.0)
                pool.memset(half[:], 0.5).then_inc(consts_set, 1)
            pool.memset(k_hl[:].bitcast(F32), 0.0)
            pool.memset(v_hl[:].bitcast(F32), 0.0).then_inc(kv_zeroed, 1)

            def split_x(t):
                pool.wait_ge(x_hi_made, t + 1)
                pool.tensor_tensor(x_lo[:, 0], x_in[:], x_hi[:, 0], ALU.subtract).then_inc(x_lo_made, 1)

            def normalise(t, b):
                pool.wait_ge(inv_made, QB * t + b + 1)
                p3 = probs[:, b % 2].rearrange("p (h s) -> p h s", s=S)
                pool.tensor_tensor(p3, p3, row_inv[:, b % 2].unsqueeze(2).to_broadcast([P, HEADS, S]),
                                   ALU.mult).then_inc(probs_ready, 1)

            def low_queries(t, m, u):
                pool.wait_ge(q_hi_made, 4 * t + m + 1)
                pool.tensor_tensor(q_lo[:, u, m], q_full[:, m % 2], q_hi[:, u, m], ALU.subtract).then_inc(q_lo_made, 1)

            def root(t):
                pool.wait_ge(var_made, t + 1)
                pool.tensor_tensor(ln[:, 1], ln[:, 0], half[:], ALU.pow).then_inc(root_made, 1)

            def affine(t, b, u):
                n = QB * t + b + 1
                pool.wait_ge(normed_made, n)
                pool.tensor_tensor(out_sb[:, u, b], out_sb[:, u, b], gb[:, 0], ALU.mult).then_inc(gamma_made, 1)
                pool.wait_ge(gamma_made, n)
                pool.tensor_tensor(out_sb[:, u, b], out_sb[:, u, b], gb[:, 1], ALU.add).then_inc(beta_made, 1)

            if second:
                for m in range(4):
                    low_queries(0, m, 0)

            def body(t, u=None):
                u = t % 2 if u is None else u
                last, more = fixed(t) and t == NT, not fixed(t) or t + 1 < NT
                affine_too = second and (not fixed(t) or t >= 2)
                if affine_too:
                    affine(t - 2, 0, u)
                    affine(t - 2, 1, u)
                if not last:
                    normalise(t, 0)
                if not second and more:
                    split_x(t + 1)
                if affine_too:
                    affine(t - 2, 2, u)
                if not last:
                    normalise(t, 1)
                if affine_too:
                    affine(t - 2, 3, u)
                if second and more:
                    low_queries(t + 1, 0, 1 - u)
                if not last:
                    normalise(t, 2)
                if second and not (fixed(t) and t == 0):
                    root(t - 1)
                if second and more:
                    low_queries(t + 1, 1, 1 - u)
                if not last:
                    normalise(t, 3)
                if second and more:
                    low_queries(t + 1, 2, 1 - u)
                    low_queries(t + 1, 3, 1 - u)

            over_tiles(pool, body, second)
            if second:
                for b in range(QB):
                    affine(NT - 1, b, (NT - 1) % 2)

        @block.scalar
        def _(act):
            if second:
                act.activation(wq_hi[:], wq_raw, ACT.Copy).then_inc(wq_hi_made, 1)

            def split_x(t):
                if not fixed(t) or t >= 1:
                    act.wait_ge(x_loaded[0], 16 * t)
                    act.wait_ge(acc_ready, head_through(t - 1, HEAD - 1))
                act.activation(x_hi[:, 0], x_in[:], ACT.Copy).then_inc(x_hi_made, 1)

            def queries(t, m, u):
                k = HEAD - 4 + m
                act.wait_ge(acc_ready, head_through(t, k))
                if second:
                    wait(act, q_lo_made, 4 * t + m - 1)
                    act.activation(q_full[:, m % 2], acc[:, k % 2], ACT.Relu, bias=bq[:, m:m + 1]).then_inc(acc_read_s, 1)
                    act.wait_ge(acc_read_s, head_reads_through("S", t, k))
                    act.activation(q_hi[:, u, m], q_full[:, m % 2], ACT.Copy).then_inc(q_hi_made, 1)
                else:
                    act.activation(q_hi[:, 0, m], acc[:, k % 2], ACT.Identity, bias=bq[:, m:m + 1]).then_inc(q_hi_made, 1)

            def exps(t, b):
                act.wait_ge(shifted, QB * t + b + 1)
                act.activation(probs[:, b % 2], probs[:, b % 2], ACT.Exp, scale=SCALE).then_inc(exp_made, 1)

            def high_probs(t, b):
                for j in range(2):
                    act.wait_ge(turned_ready, 2 * (QB * t + b) + j + 1)
                    act.activation(pT_hi[:, 4 * j:4 * j + 4, b * P:(b + 1) * P], turned[:, j],
                                   ACT.Copy).then_inc(pT_hi_made, 1)

            def values(t, c):
                act.wait_ge(acc_ready, turns_through(t, c))
                act.activation(o_hi[:, c], acc[:, c % 2], ACT.Copy).then_inc(o_hi_made, 1)

            def outputs(t, b, u):
                act.wait_ge(acc_ready, turns_through(t, 4 + b))
                if b == 0 and (not fixed(t) or t >= 3):
                    act.wait_ge(out_stored[1 - u], 16 * ((t - 1 - (1 - u)) // 2))
                act.activation(out_sb[:, 1 - u, b], acc[:, b % 2], ACT.Copy).then_inc(acc_read_s, 1)

            def standardise(t, b, u):
                act.wait_ge(ln_ready, t)
                act.activation(out_sb[:, 1 - u, b], out_sb[:, 1 - u, b], ACT.Identity, bias=ln[:, 3, b:b + 1],
                               scale=ln[:, 2, b:b + 1]).then_inc(normed_made, 1)

            if not second:
                split_x(0)
            for m in range(4):
                queries(0, m, 0)

            def body(t, u=None):
                u = t % 2 if u is None else u
                first, last = fixed(t) and t == 0, fixed(t) and t == NT
                more = not fixed(t) or t + 1 < NT
                if second:
                    if not last:
                        exps(t, 0)
                    if not first:
                        outputs(t, 0, u)
                        outputs(t, 1, u)
                    if not last:
                        exps(t, 1)
                    if not first:
                        outputs(t, 2, u)
                        outputs(t, 3, u)
                    if not last:
                        high_probs(t, 0)
                        exps(t, 2)
                    if more:
                        queries(t + 1, 0, 1 - u)
                    if not last:
                        high_probs(t, 1)
                    if more:
                        queries(t + 1, 1, 1 - u)
                    if not last:
                        exps(t, 3)
                    if more:
                        queries(t + 1, 2, 1 - u)
                    if not last:
                        high_probs(t, 2)
                    if more:
                        queries(t + 1, 3, 1 - u)
                    if not last:
                        high_probs(t, 3)
                    if not first:
                        for b in range(QB):
                            standardise(t, b, u)
                    return
                if not first:
                    high_probs(t - 1, 3)
                    values(t, 0)
                if not last:
                    exps(t, 0)
                if not first:
                    for c in range(1, 4):
                        values(t, c)
                if more:
                    split_x(t + 1)
                if not last:
                    exps(t, 1)
                    high_probs(t, 0)
                    high_probs(t, 1)
                    exps(t, 2)
                if more:
                    queries(t + 1, 0, 1 - u)
                if not last:
                    exps(t, 3)
                if more:
                    for m in range(1, 4):
                        queries(t + 1, m, 1 - u)
                if not last:
                    high_probs(t, 2)

            over_tiles(act, body, True, 2 if second else 1)

        @block.vector
        def _(dve):
            if second:
                dve.wait_ge(wq_hi_made, 1)
                dve.tensor_tensor(wq_lo[:], wq_raw, wq_hi[:], ALU.subtract).then_inc(wq_lo_made, 1)
                dve.wait_ge(consts_set, 1)
                dve.tensor_copy(ones_r[:], ones_f[:]).then_inc(ones_r_made, 1)
                dve.wait_ge(setup_in, 32)
            else:
                dve.wait_ge(x_hi_made, 1)
                dve.tensor_tensor(x_lo[:, 0], x_in[:], x_hi[:, 0], ALU.subtract).then_inc(x_lo_made, 1)

            def queries(t, m):
                dve.wait_ge(q_hi_made, 4 * t + m + 1)
                dve.scalar_tensor_tensor(out=q_lo[:, 0, m], in0=acc[:, m % 2], scalar=bq[:, m:m + 1],
                                         in1=q_hi[:, 0, m], op0=ALU.add, op1=ALU.subtract).then_inc(acc_read_v, 1)

            def query_mask(t, z, u):
                dve.wait_ge(acc_ready, head_through(t, z))
                dve.tensor_scalar(q_keep[:, u, 2 * z:2 * z + 2], acc[:, z, 0:2], 0.0, None,
                                  ALU.not_equal).then_inc(acc_read_v, 1)

            def shift(t, b, u):
                g = QB * t + b
                dve.wait_ge(scores_ready, g + 1)
                s3 = scores[:, b % 2].rearrange("p (h s) -> p h s", s=S)
                p3 = probs[:, b % 2].rearrange("p (h s) -> p h s", s=S)
                wait(dve, turned_ready, 2 * (g - 1))
                if second and u == 0 and b == 0:
                    dve.tensor_tensor(p3, s3, tri[:, 0].unsqueeze(1).to_broadcast([P, HEADS, S]),
                                      ALU.mult).then_inc(causal_made, 1)
                    dve.wait_ge(causal_made, t + 1)
                    dve.tensor_tensor(p3, p3, tri[:, 1].unsqueeze(1).to_broadcast([P, HEADS, S]),
                                      ALU.add).then_inc(causal_made, 1)
                    dve.wait_ge(causal_made, t + 2)
                    s3 = p3
                dve.tensor_reduce(row_max[:, b % 2], s3, AX_X, ALU.max).then_inc(max_made, 1)
                dve.wait_ge(max_made, g + 1)
                dve.tensor_tensor(p3, s3, row_max[:, b % 2].unsqueeze(2).to_broadcast([P, HEADS, S]),
                                  ALU.subtract).then_inc(shifted, 1)

            def invert(t, b, u):
                g = QB * t + b
                dve.wait_ge(exp_made, g + 1)
                p3 = probs[:, b % 2].rearrange("p (h s) -> p h s", s=S)
                dve.tensor_reduce(row_sum[:, b % 2], p3, AX_X, ALU.add).then_inc(sum_made, 1)
                dve.wait_ge(sum_made, g + 1)
                wait(dve, probs_ready, g - 1)
                if second:
                    dve.reciprocal(row_inv[:, b % 2], row_sum[:, b % 2]).then_inc(inv_raw, 1)
                    dve.wait_ge(inv_raw, g + 1)
                    dve.tensor_scalar(row_inv[:, b % 2], row_inv[:, b % 2], q_keep[:, u, b:b + 1], None,
                                      ALU.mult).then_inc(inv_made, 1)
                else:
                    dve.reciprocal(row_inv[:, b % 2], row_sum[:, b % 2]).then_inc(inv_made, 1)

            def low_probs(t, b):
                for j in range(2):
                    dve.wait_ge(pT_hi_made, 2 * (QB * t + b) + j + 1)
                    dve.tensor_tensor(pT_lo[:, 4 * j:4 * j + 4, b * P:(b + 1) * P], turned[:, j],
                                      pT_hi[:, 4 * j:4 * j + 4, b * P:(b + 1) * P],
                                      ALU.subtract).then_inc(pT_lo_made, 1)

            def values(t, c, u):
                if second:
                    if c == 0:
                        dve.wait_ge(res_loaded[1 - u], loads(t - 1, 1 - u))
                    dve.wait_ge(acc_ready, turns_through(t, c))
                    dve.tensor_tensor(x_res[:, 1 - u, c], acc[:, c % 2], x_res[:, 1 - u, c],
                                      ALU.add).then_inc(acc_read_v, 1)
                else:
                    dve.wait_ge(o_hi_made, 4 * (t - 1) + c + 1)
                    dve.tensor_tensor(o_lo[:, c], acc[:, c % 2], o_hi[:, c], ALU.subtract).then_inc(acc_read_v, 1)

            def residual(t, m, u):
                if m == 0:
                    dve.wait_ge(res_loaded[1 - u], loads(t - 1, 1 - u))
                dve.wait_ge(acc_ready, turns_through(t, 4 + m))
                dve.scalar_tensor_tensor(out=x_res[:, 1 - u, m], in0=acc[:, m % 2], scalar=persist["bo"][:, m:m + 1],
                                         in1=x_res[:, 1 - u, m], op0=ALU.add, op1=ALU.add).then_inc(acc_read_v, 1)

            def block_stats(t, u):
                for b in range(QB):
                    dve.wait_ge(acc_read_s, reads_through("S", t, 4 + b))
                    dve.bn_stats(stats[:, b], out_sb[:, 1 - u, b]).then_inc(stats_made, 1)

            def layer_stats(t):
                dve.wait_ge(stats_made, 2 * QB * (t - 1) + QB)
                dve.memset(wait_slot[:], 0.0)
                for b in range(QB):
                    dve.bn_aggr(mean_var[:, b], stats[:, b]).then_inc(stats_made, 1)
                dve.wait_ge(stats_made, 2 * QB * t)
                dve.tensor_scalar(ln[:, 0], mean_var[:, :, 1], float(DIM) / (DIM - 1), None,
                                  ALU.mult).then_inc(var_made, 1)

            def layer_scale(t):
                dve.wait_ge(root_made, t)
                dve.tensor_scalar(ln[:, 1], ln[:, 1], EPS, None, ALU.add).then_inc(scale_step, 1)
                dve.wait_ge(scale_step, 2 * (t - 1) + 1)
                wait(dve, normed_made, QB * (t - 1))
                dve.reciprocal(ln[:, 2], ln[:, 1]).then_inc(scale_step, 1)
                dve.wait_ge(scale_step, 2 * t)
                dve.scalar_tensor_tensor(out=ln[:, 3], in0=mean_var[:, :, 0], scalar=-1.0, in1=ln[:, 2],
                                         op0=ALU.mult, op1=ALU.mult).then_inc(ln_ready, 1)

            if second:
                for z in range(2):
                    query_mask(0, z, 0)
            else:
                for m in range(4):
                    queries(0, m)

            def body(t, u=None):
                u = t % 2 if u is None else u
                first, last = fixed(t) and t == 0, fixed(t) and t == NT
                more = not fixed(t) or t + 1 < NT
                if not first:
                    low_probs(t - 1, 3)
                if not last:
                    shift(t, 0, u)
                if not first:
                    values(t, 0, u)
                    values(t, 1, u)
                if not last:
                    invert(t, 0, u)
                if not first:
                    values(t, 2, u)
                    values(t, 3, u)
                if not last:
                    shift(t, 1, u)
                    low_probs(t, 0)
                if second:
                    if more:
                        query_mask(t + 1, 0, 1 - u)
                        query_mask(t + 1, 1, 1 - u)
                    if not last:
                        invert(t, 1, u)
                        shift(t, 2, u)
                    if not first:
                        block_stats(t, u)
                    if not last:
                        low_probs(t, 1)
                        invert(t, 2, u)
                        shift(t, 3, u)
                    if not first:
                        layer_stats(t)
                    if not last:
                        invert(t, 3, u)
                    if not first:
                        layer_scale(t)
                    if not last:
                        low_probs(t, 2)
                    return
                if not first:
                    residual(t, 0, u)
                if not last:
                    invert(t, 1, u)
                if not first:
                    residual(t, 1, u)
                if not last:
                    shift(t, 2, u)
                if not first:
                    residual(t, 2, u)
                if not last:
                    low_probs(t, 1)
                if not first:
                    residual(t, 3, u)
                if not last:
                    invert(t, 2, u)
                    shift(t, 3, u)
                if more:
                    queries(t + 1, 0)
                if not last:
                    invert(t, 3, u)
                if more:
                    for m in range(1, 4):
                        queries(t + 1, m)
                if not last:
                    low_probs(t, 2)

            over_tiles(dve, body, True)

        @block.tensor
        def _(pe):
            if second:
                pe.wait_ge(wq_lo_made, 1)
                pe.wait_ge(ones_r_made, 1)

            def query_sums(t, u):
                pe.wait_ge(x_loaded[u], 3 * loads(t, u))
                for z in range(2):
                    head_bank_free(pe, t, z)
                    for b in range(2):
                        blk = 2 * z + b
                        mm = pe.matmul(acc[:, z, b:b + 1], x_sum[:, u, blk * P:(blk + 1) * P], ones[:, 0:1],
                                       start=True, stop=True)
                    mm.then_inc(acc_ready, 1)

            def queries(t, m, u):
                k = HEAD - 4 + m
                slot = u if second else 0
                if m == 0 and not second:
                    pe.wait_ge(x_lo_made, t + 1)
                head_bank_free(pe, t, k)
                n = 0
                for c in range(C):
                    for w, x in ((wq_hi, x_hi), (wq_hi, x_lo), (wq_lo, x_hi)):
                        mm = pe.matmul(acc[:, k % 2], w[:, c, m * P:(m + 1) * P], x[:, slot, c],
                                       start=(n == 0), stop=(n == 3 * C - 1))
                        n += 1
                mm.then_inc(acc_ready, 1)

            def score(t, b, u):
                g = QB * t + b
                if b == 0 and u == 0:
                    pe.wait_ge(k_loaded, 16 * LOADS_K * (t // 2 + 1))
                slot = u if second else 0
                wait(pe, shifted, g - 1)
                for c in range(C):
                    dst = scores[:, b % 2, c * HC * S:(c + 1) * HC * S]
                    q = slice(b * P, (b + 1) * P)
                    if b == 0:
                        low_queries_made(pe, t, c)
                    start = c % 2 == 0
                    if second and start:
                        pe.matmul(scores[:, b % 2, c * HC * S:c * HC * S + HALF].rearrange("p (h s) -> p h s", s=S),
                                  ones_r[:], neg_r[:].unsqueeze(1).to_broadcast([1, HEADS // 2, S]),
                                  start=True, stop=False, skip_group_check=True)
                        start = False
                    pe.matmul(dst, q_hi[:, slot, c, q], k_hl[:, 0, c], start=start, stop=False, skip_group_check=True)
                    pe.matmul(dst, q_hi[:, slot, c, q], k_hl[:, 1, c], start=False, stop=False, skip_group_check=True)
                    mm = pe.matmul(dst, q_lo[:, slot, c, q], k_hl[:, 0, c], start=False, stop=True, skip_group_check=True)
                mm.then_inc(scores_ready, 1)

            def turn_probs(t, b):
                g = QB * t + b
                pe.wait_ge(probs_ready, g + 1)
                for j in range(2):
                    wait(pe, pT_lo_made, 2 * g + j - 1)
                    for i in range(4):
                        pair = 4 * j + i
                        mm = pe.transpose(turned[:, j, i], probs[:, b % 2, pair * P:(pair + 1) * P], ident[:])
                    mm.then_inc(turned_ready, 1)

            def values(t, c, u):
                if c == 0:
                    pe.wait_ge(pT_lo_made, 2 * QB * t)
                    pe.wait_ge(v_loaded, 16 * LOADS_V * ((t + u) // 2))
                bank_free(pe, t, c)
                n = 0
                for e in range(2):
                    for part, x in ((0, pT_hi), (0, pT_lo), (1, pT_hi)):
                        mm = pe.matmul(acc[:, c % 2], v_hl[:, part, c, e], x[:, 2 * c + e],
                                       start=(n == 0), stop=(n == 5))
                        n += 1
                mm.then_inc(acc_ready, 1)

            def project(t, m, u):
                if m == 0:
                    ended(pe, t, 3)
                bank_free(pe, t, 4 + m)
                n = 0
                for c in range(C):
                    for w, x in ((wo_hi, o_hi), (wo_hi, o_lo), (wo_lo, o_hi)):
                        mm = pe.matmul(acc[:, m % 2], w[:, c, m * P:(m + 1) * P], x[:, c],
                                       start=(n == 0), stop=(n == 3 * C - 1))
                        n += 1
                mm.then_inc(acc_ready, 1)

            def turn_out(t, b, u):
                if b == 0:
                    ended(pe, t, 3)
                bank_free(pe, t, 4 + b)
                for c in range(C):
                    mm = pe.transpose(acc[:, b % 2, c * P:(c + 1) * P], x_res[:, 1 - u, c, b * P:(b + 1) * P], ident[:])
                mm.then_inc(acc_ready, 1)

            finish = turn_out if second else project
            if second:
                query_sums(0, 0)
            for m in range(4):
                queries(0, m, 0)

            def body(t, u=None):
                u = t % 2 if u is None else u
                first, last = fixed(t) and t == 0, fixed(t) and t == NT
                more = not fixed(t) or t + 1 < NT
                if second:
                    if not last:
                        score(t, 0, u)
                        score(t, 1, u)
                    if not first:
                        for c in range(4):
                            values(t, c, u)
                    if not last:
                        score(t, 2, u)
                    if not first:
                        finish(t, 0, u)
                        finish(t, 1, u)
                    if not last:
                        turn_probs(t, 0)
                    if not first:
                        finish(t, 2, u)
                        finish(t, 3, u)
                    if more:
                        query_sums(t + 1, 1 - u)
                        queries(t + 1, 0, 1 - u)
                    if not last:
                        turn_probs(t, 1)
                        score(t, 3, u)
                    if more:
                        queries(t + 1, 1, 1 - u)
                        queries(t + 1, 2, 1 - u)
                    if not last:
                        turn_probs(t, 2)
                    if more:
                        queries(t + 1, 3, 1 - u)
                    if not last:
                        turn_probs(t, 3)
                    return
                if not last:
                    score(t, 0, u)
                if not first:
                    turn_probs(t - 1, 3)
                if not last:
                    score(t, 1, u)
                if not first:
                    for c in range(4):
                        values(t, c, u)
                if not last:
                    turn_probs(t, 0)
                if not first:
                    finish(t, 0, u)
                    finish(t, 1, u)
                if not last:
                    score(t, 2, u)
                if not first:
                    finish(t, 2, u)
                if not last:
                    turn_probs(t, 1)
                if not first:
                    finish(t, 3, u)
                if not last:
                    score(t, 3, u)
                if more:
                    for m in range(4):
                        queries(t + 1, m, 1 - u)
                if not last:
                    turn_probs(t, 2)

            over_tiles(pe, body, True)


def load_mlp_weights(sp, io, raw, j, loaded):
    w1v = io["w1"].rearrange("(c p) (j n) -> j p c n", p=P, n=P)
    sp.dma_start(raw[:, j % 2, 0].rearrange("p (c n) -> p c n", c=C), w1v[j]).then_inc(loaded, 16)
    sp.dma_start(raw[:, j % 2, 1], io["w2"][j * P:(j + 1) * P, :]).then_inc(loaded, 16)


def build_mlp(nc, io, persist, scratch):
    x_dram = scratch["x1"].rearrange("(c p) n -> p c n", p=P)
    y_dram, hi_dram, lo_dram = (scratch[k].rearrange("(c p) n -> p c n", p=P) for k in ("x2", "x2_hi", "x2_lo"))
    LAG = 2

    with ExitStack() as ctx:
        def sb(name, shape, dt=F32):
            return ctx.enter_context(nc.sbuf_tensor(f"mlp_{name}", shape, dt))

        def sem(name):
            return ctx.enter_context(nc.semaphore(f"mlp_{name}"))

        w1_hi = sb("w1_hi", [P, J, C, P], F32R)
        w1_lo = sb("w1_lo", [P, J, C, P], F32R)
        w2_hi = sb("w2_hi", [P, J, DIM], F32R)
        w2_lo = sb("w2_lo", [P, J, DIM], F32R)
        w_raw = persist["raw"]
        x = sb("x", [P, 2, C, N])
        x_hi = sb("x_hi", [P, 2, C, N], F32R)
        x_lo = sb("x_lo", [P, 2, C, N], F32R)
        g_full = sb("g_full", [P, 2, N])
        g_hi = sb("g_hi", [P, 2, N], F32R)
        g_lo = sb("g_lo", [P, 2, N], F32R)
        hid = ctx.enter_context(nc.psum_tensor("mlp_hid", [P, 4, N], F32))
        acc = ctx.enter_context(nc.psum_tensor("mlp_acc", [P, C, N], F32))

        x_sum = sb("x_sum", [P, 3, N])

        sum_step = sem("sum_step")
        x2_hi_made = sem("x2_hi_made")
        x2_lo_made = sem("x2_lo_made")
        w_loaded = [sem("w_loaded0"), sem("w_loaded1")]
        wq_loaded = sem("wq_loaded")
        w_hi_made = sem("w_hi_made")
        w_lo_made = sem("w_lo_made")
        x_loaded = [sem("x_loaded0"), sem("x_loaded1")]
        x_hi_made = sem("x_hi_made")
        x_lo_made = sem("x_lo_made")
        hid_ready = sem("hid_ready")
        gelu_made = sem("gelu_made")
        g_hi_made = sem("g_hi_made")
        g_lo_made = sem("g_lo_made")
        out_part = sem("out_part")
        out_ready = sem("out_ready")
        out_read = sem("out_read")
        stored = [sem("stored0"), sem("stored1")]
        b1, b2 = persist["b1"], persist["b2"]

        block = ctx.enter_context(nc.Block())

        @block.sync
        def _(sp):
            def load_x(t, u):
                cols = bass.ds(t * N, N) if not isinstance(t, int) else slice(t * N, (t + 1) * N)
                sp.dma_start(x[:, u], x_dram[:, :, cols]).then_inc(x_loaded[u], 16)

            load_x(0, 0)
            for j in range(2, J):
                sp.wait_ge(w_lo_made, j - 1)
                if j == 4:
                    load_x(1, 1)
                load_mlp_weights(sp, io, w_raw, j, w_loaded[j % 2])
            sp.wait_ge(w_lo_made, J)
            sp.dma_start(w_raw[:].rearrange("p a b n -> p (a b) n"),
                         io["wq1"].rearrange("(c p) n -> p c n", p=P)).then_inc(wq_loaded, 16)

            def body(t, u=None):
                u = t % 2 if u is None else u
                if not isinstance(t, int) or 1 <= t < NT - 1:
                    sp.wait_ge(stored[1 - u], 64 * ((t - 1 - (1 - u)) // 2 + 1))
                    load_x(t + 1, 1 - u)
                sp.wait_ge(out_read, C * (t + 1))
                cols = bass.ds(t * N, N) if not isinstance(t, int) else slice(t * N, (t + 1) * N)
                sp.dma_start(y_dram[:, :, cols], x[:, u]).then_inc(stored[u], 16)
                sp.wait_ge(x2_hi_made, t + 1)
                sp.dma_start(hi_dram[:, :, cols], x_hi[:, u].bitcast(F32)).then_inc(stored[u], 16)
                sp.wait_ge(x2_lo_made, t + 1)
                sp.dma_start(lo_dram[:, :, cols], x_lo[:, u].bitcast(F32)).then_inc(stored[u], 16)
                sp.wait_ge(sum_step, 3 * (t + 1))
                sp.dma_start(scratch["x2_sum"][:, cols], x_sum[:, u]).then_inc(stored[u], 16)

            over_tiles(sp, body, False)
            for u in range(2):
                sp.wait_ge(stored[u], 64 * NT // 2)
            sp.wait_ge(wq_loaded, 16)

        @block.gpsimd
        def _(pool):
            def body(t, u=None):
                u = t % 2 if u is None else u
                pool.wait_ge(out_read, C * (t + 1))
                if not isinstance(t, int) or t >= 2:
                    pool.wait_ge(stored[u], 64 * ((t - u) // 2))
                pool.tensor_tensor(x_sum[:, u], x[:, u, 0], x[:, u, 1], ALU.add).then_inc(sum_step, 1)
                wait(pool, sum_step, 3 * t)
                pool.tensor_tensor(x_sum[:, 2], x[:, u, 2], x[:, u, 3], ALU.add).then_inc(sum_step, 1)
                pool.wait_ge(sum_step, 3 * t + 2)
                pool.tensor_tensor(x_sum[:, u], x_sum[:, u], x_sum[:, 2], ALU.add).then_inc(sum_step, 1)
                if isinstance(t, int) and t == NT - 1:
                    return
                pool.wait_ge(x2_hi_made, t + 1)
                pool.tensor_tensor(x_lo[:, u], x[:, u], x_hi[:, u], ALU.subtract).then_inc(x2_lo_made, 1)

            over_tiles(pool, body, False)

        def split_x_hi(act, t, u):
            act.wait_ge(x_loaded[u], 16 * ((t - u) // 2 + 1))
            act.activation(x_hi[:, u], x[:, u], ACT.Copy).then_inc(x_hi_made, 1)

        @block.scalar
        def _(act):
            def split_w_hi(j):
                act.activation(w1_hi[:, j].rearrange("p c n -> p (c n)"), w_raw[:, j % 2, 0],
                               ACT.Copy).then_inc(w_hi_made, 1)
                act.activation(w2_hi[:, j], w_raw[:, j % 2, 1], ACT.Copy).then_inc(w_hi_made, 1)

            split_w_hi(0)
            split_w_hi(1)
            split_x_hi(act, 0, 0)

            def body(t, u=None):
                u = t % 2 if u is None else u
                for j in range(J):
                    if isinstance(t, int) and t == 0:
                        if j >= 2:
                            act.wait_ge(w_loaded[j % 2], 32 * (j // 2))
                            split_w_hi(j)
                        if j >= LAG:
                            gelu(t, j - LAG)
                    else:
                        gelu(t, j)
                        if j == LAG:
                            result_hi(t - 1, 1 - u)
                    if j == 11 and (not isinstance(t, int) or t + 1 < NT):
                        split_x_hi(act, t + 1, 1 - u)
                if isinstance(t, int) and t == 0:
                    for j in range(J - LAG, J):
                        gelu(t, j)
                if isinstance(t, int) and t == NT - 1:
                    result_hi(t, u)

            def result_hi(t, u):
                act.wait_ge(out_read, C * (t + 1))
                act.activation(x_hi[:, u], x[:, u], ACT.Copy).then_inc(x2_hi_made, 1)

            def gelu(t, j):
                n = J * t + j
                act.wait_ge(hid_ready, n + 1)
                wait(act, g_lo_made, n - 1)
                act.activation(g_full[:, j % 2], hid[:, j % 4], ACT.Gelu_apprx_tanh,
                               bias=b1[:, j:j + 1]).then_inc(gelu_made, 1)

            over_tiles(act, body, False)

        @block.vector
        def _(dve):
            def split_x_lo(t, u):
                dve.wait_ge(x_hi_made, t + 1)
                dve.tensor_tensor(x_lo[:, u], x[:, u], x_hi[:, u], ALU.subtract).then_inc(x_lo_made, 1)

            def split_hidden(t, j):
                n = J * t + j
                dve.wait_ge(gelu_made, n + 1)
                if j == 1:
                    wait(dve, out_ready, C * t)
                else:
                    wait(dve, out_part, (J - 1) * t + (j - 1 if j else 0))
                dve.tensor_copy(g_hi[:, j % 2], g_full[:, j % 2]).then_inc(g_hi_made, 1)
                dve.wait_ge(g_hi_made, n + 1)
                dve.tensor_tensor(g_lo[:, j % 2], g_full[:, j % 2], g_hi[:, j % 2], ALU.subtract).then_inc(g_lo_made, 1)

            def split_w_lo(j):
                dve.wait_ge(w_hi_made, 2 * j + 2)
                dve.tensor_tensor(w1_lo[:, j].rearrange("p c n -> p (c n)"), w_raw[:, j % 2, 0],
                                  w1_hi[:, j].rearrange("p c n -> p (c n)"), ALU.subtract)
                dve.tensor_tensor(w2_lo[:, j], w_raw[:, j % 2, 1], w2_hi[:, j], ALU.subtract).then_inc(w_lo_made, 1)

            split_w_lo(0)
            split_w_lo(1)
            split_x_lo(0, 0)

            def body(t, u=None):
                u = t % 2 if u is None else u
                for j in range(J):
                    if isinstance(t, int) and t == 0:
                        if j >= 2:
                            split_w_lo(j)
                        if j >= LAG:
                            split_hidden(t, j - LAG)
                    else:
                        split_hidden(t, j)
                    if j == 11 and (not isinstance(t, int) or t + 1 < NT):
                        split_x_lo(t + 1, 1 - u)
                if isinstance(t, int) and t == 0:
                    for j in range(J - LAG, J):
                        split_hidden(t, j)
                for m in range(C):
                    dve.wait_ge(out_ready, C * t + m + 1)
                    dve.scalar_tensor_tensor(out=x[:, u, m], in0=acc[:, m], scalar=b2[:, m:m + 1], in1=x[:, u, m],
                                             op0=ALU.add, op1=ALU.add).then_inc(out_read, 1)

            over_tiles(dve, body, False)
            u = (NT - 1) % 2
            dve.wait_ge(x2_hi_made, NT)
            dve.wait_ge(x2_lo_made, NT - 1)
            dve.tensor_tensor(x_lo[:, u], x[:, u], x_hi[:, u], ALU.subtract).then_inc(x2_lo_made, 1)

        @block.tensor
        def _(pe):
            def first(t, j, u):
                if j == 0:
                    pe.wait_ge(x_lo_made, t + 1)
                if isinstance(t, int) and t == 0:
                    pe.wait_ge(w_lo_made, j + 1)
                wait(pe, gelu_made, J * t + j - 3)
                n = 0
                for c in range(C):
                    for w, xs in ((w1_hi, x_hi), (w1_hi, x_lo), (w1_lo, x_hi)):
                        mm = pe.matmul(hid[:, j % 4], w[:, j, c], xs[:, u, c], start=(n == 0), stop=(n == 3 * C - 1))
                        n += 1
                mm.then_inc(hid_ready, 1)

            def then(t, j, u):
                pe.wait_ge(g_lo_made, J * t + j + 1)
                for m in range(C):
                    if j == 0:
                        wait(pe, out_read, C * (t - 1) + m + 1)
                    for n, (w, g) in enumerate(((w2_hi, g_hi), (w2_hi, g_lo), (w2_lo, g_hi))):
                        mm = pe.matmul(acc[:, m], w[:, j, m * P:(m + 1) * P], g[:, j % 2],
                                       start=(j == 0 and n == 0), stop=(j == J - 1 and n == 2))
                    if j == J - 1:
                        mm.then_inc(out_ready, 1)
                    elif m == C - 1:
                        mm.then_inc(out_part, 1)

            def body(t, u=None):
                u = t % 2 if u is None else u
                for j in range(J + LAG):
                    if j < J:
                        first(t, j, u)
                    if j >= LAG:
                        then(t, j - LAG, u)

            over_tiles(pe, body, False)


def build(nc, io):
    with ExitStack() as ctx:
        def sb(name, shape, dt=F32):
            return ctx.enter_context(nc.sbuf_tensor(name, shape, dt))

        bias = sb("bias", [P, 6 * C + J])
        raw = sb("raw", [P, 2, 2, DIM])
        persist = {"bias": bias, "ident": sb("ident", [P, P]), "raw": raw}
        cols = [bias[:, C * i:C * (i + 1)] for i in range(6)]
        persist["bq"] = [cols[0], cols[1]]
        persist["bk"] = [cols[2], cols[3]]
        persist["bo"], persist["b2"] = cols[4], cols[5]
        persist["b1"] = bias[:, 6 * C:6 * C + J]
        scratch = {
            "k": nc.dram_tensor("k_scratch", [2, 2, C, P, BS], F32, kind="Internal").ap(),
            "v": nc.dram_tensor("v_scratch", [2, 2, BS, DIM], F32, kind="Internal").ap(),
            "x1": nc.dram_tensor("x1_scratch", [DIM, B * TOK], F32, kind="Internal").ap(),
            "neg": nc.dram_tensor("neg_scratch", [1, BS], F32, kind="Internal").ap(),
            "x2_hi": nc.dram_tensor("x2_hi_scratch", [DIM, B * TOK], F32, kind="Internal").ap(),
            "x2_lo": nc.dram_tensor("x2_lo_scratch", [DIM, B * TOK], F32, kind="Internal").ap(),
            "x2_sum": nc.dram_tensor("x2_sum_scratch", [P, B * TOK], F32, kind="Internal").ap(),
            "x2": nc.dram_tensor("x2_scratch", [DIM, B * TOK], F32, kind="Internal").ap(),
        }
        with ExitStack() as early:
            for name in ("wq_hi", "wq_lo", "wo_hi", "wo_lo"):
                persist[name] = early.enter_context(nc.sbuf_tensor(name, [P, C, DIM], F32R))
            persist["x_in"] = early.enter_context(nc.sbuf_tensor("x_in", [P, C, N], F32))
            build_keys(nc, io, persist, scratch)
            build_attention(nc, io, persist, scratch, 0)
        build_mlp(nc, io, persist, scratch)
        build_attention(nc, io, persist, scratch, 1)


def kernel(x, ctx_1024, L0_xattn_Wq, L0_xattn_bq, L0_xattn_Wk, L0_xattn_bk, L0_xattn_Wv, L0_xattn_bv,
           L0_xattn_Wo, L0_xattn_bo, L0_xattn_W1, L0_xattn_b1, L0_xattn_W2, L0_xattn_b2,
           L1_xattn_Wq, L1_xattn_bq, L1_xattn_Wk, L1_xattn_bk, L1_xattn_Wv, L1_xattn_bv,
           L1_xattn_gamma, L1_xattn_beta):
    import numpy as np
    import concourse.bacc as bacc
    from concourse.bass_utils import run_bass_kernel_spmd

    def by_chunk(v):
        return np.asarray(v).reshape(-1, P).T

    def rows(*vs):
        return np.ascontiguousarray(np.broadcast_to(np.stack([np.asarray(v) for v in vs])[None], (P, len(vs), DIM)))

    allowed = (np.arange(P)[:, None] >= np.arange(S)[None, :]).astype(np.float32)
    arrays = {
        "xT": np.asarray(x).reshape(B * TOK, DIM).T,
        "ctxT": np.asarray(ctx_1024).reshape(BS, DIM).T,
        "wq0": L0_xattn_Wq, "wk0": L0_xattn_Wk, "wv0": L0_xattn_Wv, "wo0": L0_xattn_Wo,
        "w1": L0_xattn_W1, "w2": L0_xattn_W2,
        "wq1": np.asarray(L1_xattn_Wq).T, "wk1": np.asarray(L1_xattn_Wk).T, "wv1": np.asarray(L1_xattn_Wv).T,
        "bias": np.concatenate([by_chunk(v) for v in (L0_xattn_bq, L1_xattn_bq, L0_xattn_bk, L1_xattn_bk,
                                                      L0_xattn_bo, L0_xattn_b2, L0_xattn_b1)], axis=1),
        "bv": rows(L0_xattn_bv, L1_xattn_bv),
        "gb": rows(L1_xattn_gamma, L1_xattn_beta),
        "ident": np.eye(P, dtype=np.float32),
        "tri": np.stack([allowed, np.where(allowed > 0, 0.0, NEG).astype(np.float32)], axis=1),
    }
    arrays = {f"in_{k}": np.ascontiguousarray(v) for k, v in arrays.items()}
    nc = bacc.Bacc("TRN2", target_bir_lowering=False, num_devices=1)
    io = {k[3:]: nc.dram_tensor(k, a.shape, mybir.dt.from_np(a.dtype), kind="ExternalInput").ap()
          for k, a in arrays.items()}
    io["out"] = nc.dram_tensor("out", (B * TOK, DIM), F32, kind="ExternalOutput").ap()
    build(nc, io)
    r = run_bass_kernel_spmd(nc, [arrays], core_ids=[0])
    return r.results[0]["out"].reshape(B, TOK, DIM)
```
